# Optimizing a Trainium2 kernel written in Bass

```python
import numpy as np
import jax
import jax.numpy as jnp

def _softmax(x, axis=-1):
    return jax.nn.softmax(x, axis=axis)

def _gelu(x):
    return jax.nn.gelu(x, approximate=True)

def _silu(x):
    return jax.nn.silu(x)

def _sigmoid(x):
    return jax.nn.sigmoid(x)

def _layernorm(x, axis=-1, eps=1e-05):
    m = jnp.mean(x, axis=axis, keepdims=True)
    v = jnp.var(x, axis=axis, keepdims=True)
    return (x - m) / jnp.sqrt(v + eps)

def _scatter_add(tgt, idx, src, axis=0):
    return tgt.at[idx].add(src)

def _segment_sum(src, seg, n):
    return jax.ops.segment_sum(src, seg, n)
kernel_name = 'mk_dlrm_tower_d1_rec_r8_1f5de7'

def setup_inputs(seed: int=0):
    np.random.seed(seed)
    _w = jnp.asarray

    def _rec_inputs():
        import jax
        import jax.numpy as jnp
        _tk = jax.random.key(seed)
        dense_ctx = jax.random.normal(jax.random.fold_in(_tk, 190), (2048, 16), jnp.float32)
        ids = jnp.stack([jax.random.randint(jax.random.fold_in(_tk, 200 + f), (2048,), 0, v, jnp.int32) for f, v in enumerate([125000, 1250, 125000, 1000, 12500, 125000, 1000, 1250, 125000, 1000, 12500, 1000, 12500, 1250, 1250, 1250])], axis=1)
        tbl_0 = 0.05 * jax.random.normal(jax.random.fold_in(_tk, 500 + 0), (125000, 16), jnp.float32)
        tbl_1 = 0.05 * jax.random.normal(jax.random.fold_in(_tk, 500 + 1), (1250, 16), jnp.float32)
        tbl_2 = 0.05 * jax.random.normal(jax.random.fold_in(_tk, 500 + 2), (125000, 16), jnp.float32)
        tbl_3 = 0.05 * jax.random.normal(jax.random.fold_in(_tk, 500 + 3), (1000, 16), jnp.float32)
        tbl_4 = 0.05 * jax.random.normal(jax.random.fold_in(_tk, 500 + 4), (12500, 16), jnp.float32)
        tbl_5 = 0.05 * jax.random.normal(jax.random.fold_in(_tk, 500 + 5), (125000, 16), jnp.float32)
        tbl_6 = 0.05 * jax.random.normal(jax.random.fold_in(_tk, 500 + 6), (1000, 16), jnp.float32)
        tbl_7 = 0.05 * jax.random.normal(jax.random.fold_in(_tk, 500 + 7), (1250, 16), jnp.float32)
        tbl_8 = 0.05 * jax.random.normal(jax.random.fold_in(_tk, 500 + 8), (125000, 16), jnp.float32)
        tbl_9 = 0.05 * jax.random.normal(jax.random.fold_in(_tk, 500 + 9), (1000, 16), jnp.float32)
        tbl_10 = 0.05 * jax.random.normal(jax.random.fold_in(_tk, 500 + 10), (12500, 16), jnp.float32)
        tbl_11 = 0.05 * jax.random.normal(jax.random.fold_in(_tk, 500 + 11), (1000, 16), jnp.float32)
        tbl_12 = 0.05 * jax.random.normal(jax.random.fold_in(_tk, 500 + 12), (12500, 16), jnp.float32)
        tbl_13 = 0.05 * jax.random.normal(jax.random.fold_in(_tk, 500 + 13), (1250, 16), jnp.float32)
        tbl_14 = 0.05 * jax.random.normal(jax.random.fold_in(_tk, 500 + 14), (1250, 16), jnp.float32)
        tbl_15 = 0.05 * jax.random.normal(jax.random.fold_in(_tk, 500 + 15), (1250, 16), jnp.float32)
        _rk = jax.random.fold_in(_tk, 7)
        r_x0 = -0.000233584 + 0.999828 * jax.random.normal(jax.random.fold_in(_rk, 101), (2048, 39, 16), jnp.float32)
        W_top1 = 0.0606339 * jax.random.normal(jax.random.fold_in(_tk, 801), (272, 512), jnp.float32)
        W_top2 = 0.0441942 * jax.random.normal(jax.random.fold_in(_tk, 802), (512, 256), jnp.float32)
        W_top3 = 0.0625 * jax.random.normal(jax.random.fold_in(_tk, 803), (256, 1), jnp.float32)
        b_top1 = jnp.zeros((512,), jnp.float32)
        b_top2 = jnp.zeros((256,), jnp.float32)
        return (dense_ctx, ids, tbl_0, tbl_1, tbl_2, tbl_3, tbl_4, tbl_5, tbl_6, tbl_7, tbl_8, tbl_9, tbl_10, tbl_11, tbl_12, tbl_13, tbl_14, tbl_15, r_x0, W_top1, b_top1, W_top2, b_top2, W_top3)
    dense_ctx, ids, tbl_0, tbl_1, tbl_2, tbl_3, tbl_4, tbl_5, tbl_6, tbl_7, tbl_8, tbl_9, tbl_10, tbl_11, tbl_12, tbl_13, tbl_14, tbl_15, r_x0, W_top1, b_top1, W_top2, b_top2, W_top3 = _rec_inputs()

    def _L0_rec_setup():
        import jax, jax.numpy as jnp
        import numpy as np
        B, S, F, D, K = (1024, 16, 39, 16, 16)
        key = jax.random.key(seed)
        k1, k2, k3, k4, k5 = jax.random.split(key, 5)
        xl = jax.random.normal(k1, (B, S, D), dtype=jnp.float32)
        x0 = jax.random.normal(k2, (B, F, D), dtype=jnp.float32)
        w = jnp.broadcast_to(jnp.eye(D, dtype=jnp.float32), (K, D, D)) + 0.02 * jax.random.normal(k3, (K, D, D), dtype=jnp.float32)
        alpha = jnp.ones((S * F, K), dtype=jnp.float32) + 0.02 * jax.random.normal(k4, (S * F, K), dtype=jnp.float32)
        hv = jnp.ones((K, D, 1), dtype=jnp.float32) + 0.02 * jax.random.normal(k5, (K, D, 1), dtype=jnp.float32)
        return {'xl': xl, 'x0': x0, 'w': w, 'alpha': alpha, 'hv': hv}
    _L0_rec_all = _L0_rec_setup()
    _L0_rec_in = {k: v for k, v in _L0_rec_all.items() if k in ('w', 'alpha', 'hv')}
    del _L0_rec_all
    return {'dense_ctx': dense_ctx, 'ids': ids, 'tbl_0': tbl_0, 'tbl_1': tbl_1, 'tbl_2': tbl_2, 'tbl_3': tbl_3, 'tbl_4': tbl_4, 'tbl_5': tbl_5, 'tbl_6': tbl_6, 'tbl_7': tbl_7, 'tbl_8': tbl_8, 'tbl_9': tbl_9, 'tbl_10': tbl_10, 'tbl_11': tbl_11, 'tbl_12': tbl_12, 'tbl_13': tbl_13, 'tbl_14': tbl_14, 'tbl_15': tbl_15, 'r_x0': r_x0, 'W_top1': W_top1, 'b_top1': b_top1, 'W_top2': W_top2, 'b_top2': b_top2, 'W_top3': W_top3, 'L0_rec_w': _L0_rec_in['w'], 'L0_rec_alpha': _L0_rec_in['alpha'], 'L0_rec_hv': _L0_rec_in['hv']}

def reference(dense_ctx, ids, tbl_0, tbl_1, tbl_2, tbl_3, tbl_4, tbl_5, tbl_6, tbl_7, tbl_8, tbl_9, tbl_10, tbl_11, tbl_12, tbl_13, tbl_14, tbl_15, r_x0, W_top1, b_top1, W_top2, b_top2, W_top3, L0_rec_w, L0_rec_alpha, L0_rec_hv):
    import jax
    import jax.numpy as jnp

    def _L0_rec_ref(xl, x0, w, alpha, hv):
        import jax, jax.numpy as jnp
        import numpy as np
        B, S, F, D, K = (1024, 16, 39, 16, 16)
        b, s, d = xl.shape
        f = x0.shape[1]
        A = jnp.repeat(x0, s, axis=1)
        Bm = jnp.repeat(xl, f, axis=2).reshape(b, s * f, d)
        out = jnp.einsum('bnh,bnd,nk,khd,kd->bkh', A, Bm, alpha, w, hv[..., 0])
        return out
    e = jnp.stack([tbl_0[ids[:, 0]], tbl_1[ids[:, 1]], tbl_2[ids[:, 2]], tbl_3[ids[:, 3]], tbl_4[ids[:, 4]], tbl_5[ids[:, 5]], tbl_6[ids[:, 6]], tbl_7[ids[:, 7]], tbl_8[ids[:, 8]], tbl_9[ids[:, 9]], tbl_10[ids[:, 10]], tbl_11[ids[:, 11]], tbl_12[ids[:, 12]], tbl_13[ids[:, 13]], tbl_14[ids[:, 14]], tbl_15[ids[:, 15]]], axis=1)
    z = _L0_rec_ref(e, r_x0, L0_rec_w, L0_rec_alpha, L0_rec_hv)
    z = z.reshape(z.shape[0], -1)
    h = jnp.concatenate([z, dense_ctx], axis=1)
    h = jnp.maximum(h @ W_top1 + b_top1, 0.0)
    h = jnp.maximum(h @ W_top2 + b_top2, 0.0)
    y = h @ W_top3
    return y

_drawn_inputs = setup_inputs


def setup_inputs(seed=0):
    import zlib

    import numpy as np

    out = dict(_drawn_inputs(seed))
    spreads = {'b_top1': (0.0, 0.1), 'b_top2': (0.0, 0.1)}
    factors = {}
    for name, (base, spread) in spreads.items():
        noise = np.random.default_rng([zlib.crc32(name.encode()), seed]).standard_normal(out[name].shape)
        drawn = base * np.exp(spread * noise) if base else spread * noise
        out[name] = jnp.asarray(drawn.astype(out[name].dtype))
    for name, factor in factors.items():
        out[name] = (out[name] * factor).astype(out[name].dtype)
    return out
```

```python
from contextlib import ExitStack

import concourse.bass as bass
import numpy as np
from concourse import mybir

F32 = mybir.dt.float32
I32 = mybir.dt.int32
ALU = mybir.AluOpType
ACT = mybir.ActivationFunctionType

P = 128
BATCH = 2048
TABLES = 16
F = 39
FP = 40
D = 16
K = 16
H = 16
EMB = TABLES * D
R = 8
FC = P // R
TB = 256
BT = TB // P
NT = BATCH // TB
HALF = 8
QUADS = 4
STEPS = 10
NPROD = 4
N1, N2 = 512, 256
PRODS = 6
USES = 4
CHUNK_A, CHUNK_B, CHUNK_C = range(3)
CHUNKS = [(CHUNK_A, 0, FC), (CHUNK_B, FC, FC), (CHUNK_C, 2 * FC, F - 2 * FC)]
KINDS = [(zt, chunk, odd) for chunk in (CHUNK_A, CHUNK_B) for zt in range(2) for odd in range(2)]
KINDS += [(zt, CHUNK_C, None) for zt in range(2)]
MLP_AT = {1: "L1 0", 2: "L1 1", 3: "L1 2", 4: "L1 3", 6: "L2 0", 7: "L2 1", 9: "L3"}


def first_embedding(f):
    first, count, m, step = next(r for r in RUNS if r[0] <= f < r[0] + r[1])
    return m + step * (f - first)


def feature_runs():
    def fits(f, m):
        return 256 * f // F >= m >= 0 and (256 * f + 255) // F < m + R <= EMB
    runs, f = [], 0
    while f < F:
        end = min(F, FC * (f // FC + 1))
        best = (f, 0, 0, 0)
        for step in range(R):
            for m in range(256 * f // F, max(0, 256 * f // F - 2) - 1, -1):
                n = 0
                while f + n < end and fits(f + n, m + step * n):
                    n += 1
                if n > best[1]:
                    best = (f, n, m, step)
        runs.append(best)
        f += best[1]
    return runs


RUNS = feature_runs()


def constants():
    ident = np.eye(P, dtype=np.float32)
    groups = FP // 8
    below = np.zeros((P, groups, D), np.float32)
    above = np.zeros((P, groups, D), np.float32)
    slot = np.zeros((P, groups, 2, 8 * R), np.float32)
    for n in range(16 * F):
        g, row, f = n // P, n % P, n // 16
        low, high = 16 * n // F, (16 * n + 15) // F
        for d in range(D):
            (below if (16 * n + d) // F == low else above)[row, g, d] = 1.0
        for side, m in enumerate((low, high)):
            slot[row, g, side, R * (f % 8) + m - first_embedding(f)] = 1.0
    block = np.kron(np.eye(8, dtype=np.float32), np.ones((H, 1), np.float32))
    return {"ident": ident, "below": below, "above": above, "slot": slot, "block": block}


def interaction_tower(nc, dense_ctx, ids, tables, x0, w_top1, b_top1, w_top2, b_top2, w_top3,
                      w, alpha, hv, consts, const_at, out):
    G = FP // 8
    NALPHA = 16 * F
    with ExitStack() as ctx:
        def sb(name, shape, dt=F32):
            return ctx.enter_context(nc.sbuf_tensor(name, shape, dt))

        def bank(name, shape):
            return ctx.enter_context(nc.psum_tensor(name, shape, F32))

        def sem(name):
            return ctx.enter_context(nc.semaphore(name))

        const = sb("const", [P, consts.shape[1]])

        def const_view(name, *dims):
            a, n = const_at[name]
            v = const[:, a:a + n]
            if len(dims) == 2:
                return v.rearrange("p (a b) -> p a b", a=dims[0])
            if len(dims) == 3:
                return v.rearrange("p (a b c) -> p a b c", a=dims[0], b=dims[1])
            return v

        ident = const_view("ident")
        below = const_view("below", G, D)
        above = const_view("above", G, D)
        slot = const_view("slot", G, 2, 8 * R)
        block_mask = const_view("block")
        w1z = sb("w1z", [P, 2, N1])
        w1d = sb("w1d", [D, N1])
        w2 = sb("w2", [P, N1 // P, N2])
        w3 = sb("w3", [P, N2 // P])
        b1 = sb("b1", [P, N1 // P])
        b2 = sb("b2", [P, N2 // P])
        hv_col = sb("hv_col", [P, 2])
        w_rows = sb("w_rows", [P, 2, D])
        alpha_rows = sb("alpha_rows", [P, G, K])
        alpha_cut = sb("alpha_cut", [P, 2, G, K, D])
        w_diag = sb("w_diag", [P, 2, 8, D])
        whv_diag = sb("whv_diag", [P, 2, P])
        alpha_slot = sb("alpha_slot", [P, 2, FP * R])
        m_ab = sb("m_ab", [P, 2, H, 32])
        m_c = sb("m_c", [P, H // 2, 32])
        dense_in = sb("dense_in", [P, NT * BT, D])
        dense_t = sb("dense_t", [D, NT, TB])
        ids_in = sb("ids_in", [P, 2, BT, TABLES], I32)
        x_in = sb("x_in", [P, 2, BT, F * H])
        emb = sb("emb", [P, 2, BT, EMB])
        emb_slot = sb("emb_slot", [P, 2, BT, FP * R])
        prod_ab = sb("prod_ab", [P, 2, 2, BT, H, P])
        prod_c = sb("prod_c", [P, 2, BT, H, P // 2])
        prod_t = sb("prod_t", [P, NPROD, QUADS, TB])
        z_sb = sb("z_sb", [P, 2, 2, TB])
        h1 = sb("h1", [P, N1 // P, TB])
        h2 = sb("h2", [P, N2 // P, TB])
        y = sb("y", [P, 2, TB // QUADS])

        turned = [bank(f"turned{i}", [P, QUADS, TB]) for i in range(2)]
        z_ps = [bank(f"z_ps{i}", [P, 512]) for i in range(2)]
        shared = [bank(f"shared{i}", [P, 2, TB]) for i in range(2)]

        small_loaded = sem("small_loaded")
        const_loaded = sem("const_loaded")
        weights_loaded = sem("weights_loaded")
        ids_loaded = [sem(f"ids_loaded{i}") for i in range(2)]
        x_loaded = [sem(f"x_loaded{i}") for i in range(2)]
        gathered = [sem(f"gathered{i}") for i in range(2)]
        gather_turn = sem("gather_turn")
        cleared = sem("cleared")
        setup_dve = sem("setup_dve")
        setup_pe = sem("setup_pe")
        setup_act = sem("setup_act")
        slotted = sem("slotted")
        prod_ready = sem("prod_ready")
        turned_full = sem("turned_full")
        copied = sem("copied")
        z_step = sem("z_step")
        z_drained = sem("z_drained")
        shared_full = sem("shared_full")
        shared_drained = sem("shared_drained")
        y_stored = [sem(f"y_stored{i}") for i in range(2)]

        out_rows = out.rearrange("(t q n) o -> t q (n o)", t=NT, q=QUADS)
        ids_rows = ids.rearrange("(t c p) s -> t p c s", c=BT, p=P)
        x_rows = x0.rearrange("(t c p) f h -> t p c (f h)", c=BT, p=P)
        dense_rows = dense_ctx.rearrange("(c p) s -> p c s", p=P)
        w1_rows = w_top1[0:K * H, :].rearrange("(k z hh) n -> z hh k n", z=2, hh=HALF)

        block = ctx.enter_context(nc.Block())

        def windows(values, m, count, step):
            (pstep, pn), (cstep, cn), _ = values.ap
            return bass.AP(values.tensor, values.offset + m, [[pstep, pn], [cstep, cn], [step, count], [1, R]])

        def at_tile(rows, t):
            if isinstance(t, int):
                return rows[t]
            return rows[bass.ds(t, 1)].squeeze(0)

        def shared_flat(i):
            return shared[i][:].rearrange("p a b -> p (a b)")

        @block.sync
        def _(sp):
            def load(k, p, again):
                t = 2 * k + p
                if again:
                    sp.wait_ge(gathered[p], 16 * TABLES * BT * k)
                sp.dma_start(ids_in[:, p], at_tile(ids_rows, t)).then_inc(ids_loaded[p], 16)
                if again:
                    sp.wait_ge(prod_ready, PRODS * (t - 1))
                sp.dma_start(x_in[:, p], at_tile(x_rows, t)).then_inc(x_loaded[p], 16)

            load(0, 0, False)
            load(0, 1, False)
            with sp.Fori(1, NT // 2) as k:
                load(k, 0, True)
                load(k, 1, True)

        @block.gpsimd
        def _(pool):
            def gather(k, p, again):
                t = 2 * k + p
                pool.wait_ge(ids_loaded[p], 16 * (k + 1))
                if again:
                    pool.wait_ge(gathered[p], 16 * TABLES * BT * k)
                    pool.wait_ge(slotted, len(RUNS) * (t - 1))
                    pool.sem_inc(gather_turn, 1)
                for c in range(BT):
                    for s in range(TABLES):
                        pool.indirect_dma_start(
                            emb[:, p, c, D * s:D * (s + 1)], None, tables[s],
                            bass.IndirectOffsetOnAxis(ids_in[:, p, c, s:s + 1], 0)).then_inc(gathered[p], 16)

            gather(0, 0, False)
            gather(0, 1, False)
            with pool.Fori(1, NT // 2) as k:
                gather(k, 0, True)
                gather(k, 1, True)

        @block.vector
        def _(dve):
            nc.vector.memset(alpha_rows[:], 0.0).then_inc(cleared, 1)
            nc.vector.memset(prod_c[:], 0.0).then_inc(cleared, 1)
            nc.vector.memset(m_ab[:], 0.0).then_inc(cleared, 1)
            nc.vector.memset(m_c[:], 0.0).then_inc(cleared, 1)
            dve.wait_ge(small_loaded, 16 * 6)
            dve.wait_ge(const_loaded, 16)
            for z in range(2):
                nc.vector.tensor_tensor(
                    w_diag[:, z], w_rows[:, z].unsqueeze(1).broadcast_to([P, 8, D]),
                    block_mask.unsqueeze(2).broadcast_to([P, 8, D]), ALU.mult).then_inc(setup_dve, 1)
            for side, mask in enumerate((below, above)):
                nc.vector.tensor_tensor(
                    alpha_cut[:, side], alpha_rows[:].unsqueeze(3).broadcast_to([P, G, K, D]),
                    mask.unsqueeze(2).broadcast_to([P, G, K, D]), ALU.mult).then_inc(setup_dve, 1)

            def products(k, p, again):
                t = 2 * k + p
                dve.wait_ge(gathered[p], 16 * TABLES * BT * (k + 1))
                if again:
                    dve.wait_ge(prod_ready, PRODS * (t - 1))
                for f, count, m, step in RUNS:
                    nc.vector.tensor_copy(
                        emb_slot[:, p, :, R * f:R * (f + count)].rearrange("p c (f r) -> p c f r", r=R),
                        windows(emb[:, p], m, count, step)).then_inc(slotted, 1)
                dve.wait_ge(x_loaded[p], 16 * (k + 1))
                dve.wait_ge(slotted, len(RUNS) * (t + 1))
                for chunk, feature, count in CHUNKS:
                    if again:
                        dve.wait_ge(turned_full, STEPS * (t - 2) + min(STEPS, 4 * (chunk + 1)))
                    for c in range(BT):
                        to = prod_c[:, p, c, :, 0:R * count] if chunk == CHUNK_C else prod_ab[:, p, chunk, c]
                        rows = x_in[:, p, c].rearrange("p (f h) -> p h f", h=H)[:, :, feature:feature + count]
                        slots = emb_slot[:, p, c, R * feature:R * (feature + count)]
                        nc.vector.tensor_tensor(
                            to.rearrange("p h (f r) -> p h f r", r=R),
                            rows.unsqueeze(3).broadcast_to([P, H, count, R]),
                            slots.unsqueeze(1).broadcast_to([P, H, R * count]).rearrange("p h (f r) -> p h f r", r=R),
                            ALU.mult).then_inc(prod_ready, 1)

            products(0, 0, False)
            products(0, 1, False)
            with dve.Fori(1, NT // 2) as k:
                products(k, 0, True)
                products(k, 1, True)

        @block.scalar
        def _(act):
            with nc.allow_non_contiguous_dma(reason="small vectors, one element to a partition"):
                act.dma_start(const[:], consts).then_inc(const_loaded, 16)
                act.wait_ge(cleared, 1)
                act.dma_start(alpha_rows[:, 0:NALPHA // P],
                              alpha[0:P * (NALPHA // P), :].rearrange("(g p) k -> p g k", p=P)).then_inc(small_loaded, 16)
                act.dma_start(alpha_rows[0:NALPHA % P, NALPHA // P],
                              alpha[P * (NALPHA // P):NALPHA, :]).then_inc(small_loaded, 16)
                act.dma_start(w_rows[:], w.rearrange("(z k) h d -> z (k h) d", z=2).rearrange("z q d -> q z d")).then_inc(small_loaded, 16)
                act.dma_start(dense_in[:], dense_rows).then_inc(small_loaded, 16)
                hv_rows = hv.rearrange("(z k) d o -> z (k d) o", z=2)
                for z in range(2):
                    act.dma_start(hv_col[:, z:z + 1], hv_rows[z]).then_inc(small_loaded, 16)
                for z in range(2):
                    for hh in range(HALF):
                        act.dma_start(w1z[K * hh:K * (hh + 1), z], w1_rows[z, hh]).then_inc(weights_loaded, 16)
                act.dma_start(w1d[:], w_top1[K * H:K * H + D, :]).then_inc(weights_loaded, 16)
                act.dma_start(w2[:], w_top2.rearrange("(m p) n -> p m n", p=P)).then_inc(weights_loaded, 16)
                act.dma_start(w3[:], w_top3.rearrange("(m p) o -> p (m o)", p=P)).then_inc(weights_loaded, 16)
                act.dma_start(b1[:], b_top1.rearrange("(m p) -> p m", p=P)).then_inc(weights_loaded, 16)
                act.dma_start(b2[:], b_top2.rearrange("(m p) -> p m", p=P)).then_inc(weights_loaded, 16)

            act.wait_ge(setup_pe, 1)
            act.wait_ge(small_loaded, 16 * 6)
            for z in range(2):
                nc.scalar.activation(whv_diag[:, z], z_ps[0][:, P * z:P * (z + 1)], ACT.Copy,
                                     scale=hv_col[:, z:z + 1]).then_inc(setup_act, 1)
            act.wait_ge(shared_full, 2)
            for z in range(2):
                nc.scalar.activation(alpha_slot[:, z], shared_flat(z)[:, 0:FP * R], ACT.Copy).then_inc(shared_drained, 1)
            act.wait_ge(setup_pe, 2)
            act.wait_ge(cleared, 4)
            m_view = [z_ps[0][:, 0:256], z_ps[0][:, 256:512], z_ps[1][:, 0:256]]
            for odd in range(2):
                cols = slice(K * odd, K * (odd + 1))
                for chunk in (CHUNK_A, CHUNK_B):
                    nc.scalar.activation(
                        m_ab[:, chunk, odd::2, cols],
                        m_view[chunk].rearrange("p (k h) -> p h k", h=H)[:, odd::2, :], ACT.Copy).then_inc(setup_act, 1)
                rows = slice(64 * odd, 64 * (odd + 1))
                nc.scalar.activation(
                    m_c[rows, :, cols],
                    m_view[CHUNK_C].rearrange("p (k h) -> p h k", h=H)[rows, odd::2, :], ACT.Copy).then_inc(setup_act, 1)
            act.wait_ge(setup_pe, 3)
            for i in range(2):
                nc.scalar.activation(dense_t[:].rearrange("p t n -> p (t n)")[:, 4 * TB * i:4 * TB * (i + 1)],
                                     turned[i][0:D].rearrange("p q n -> p (q n)"), ACT.Copy).then_inc(setup_act, 1)
            act.wait_ge(weights_loaded, 16 * 21)

            def copy_products(t, p, s, first):
                n = STEPS * t + s
                act.wait_ge(turned_full, n + 1)
                if not first or s >= NPROD:
                    act.wait_ge(z_step, n - NPROD + 1)
                nc.scalar.activation(prod_t[:, (STEPS * p + s) % NPROD], turned[s % 2][:], ACT.Copy).then_inc(copied, 1)

            def drain_z(t, p, zt):
                act.wait_ge(z_step, STEPS * t + STEPS - 1 + zt)
                nc.scalar.activation(z_sb[:, p, zt], z_ps[zt][:, 0:TB], ACT.Copy).then_inc(z_drained, 1)

            def drain_layer(use, source, hidden, bias, m):
                act.wait_ge(shared_full, use + 1)
                for i in range(2):
                    last = nc.scalar.activation(hidden[:, m + i], source[:, i], ACT.Relu,
                                                bias=bias[:, m + i:m + i + 1])
                last.then_inc(shared_drained, 1)

            def store_y(use, k, p, again):
                act.wait_ge(shared_full, use + 1)
                if again:
                    act.wait_ge(y_stored[p], 16 * k)
                nc.scalar.activation(y[:, p], shared[1][:, 0, 0:TB // QUADS], ACT.Copy).then_inc(shared_drained, 1)
                act.wait_ge(shared_drained, use + 1)
                act.dma_start(at_tile(out_rows, 2 * k + p), y[0:97:32, p]).then_inc(y_stored[p], 16)

            def mlp_drain(what, k, p, again):
                use = USES * (2 * k + p) + 2
                if what == "L1 1":
                    drain_layer(use, shared[0], h1, b1, 0)
                elif what == "L1 3":
                    drain_layer(use + 1, shared[1], h1, b1, 2)
                elif what == "L2 1":
                    drain_layer(use + 2, shared[0], h2, b2, 0)
                elif what == "L3":
                    store_y(use + 3, k, p, again)

            def tile(k, p, mlp, again=False):
                t = 2 * k + p
                bk, bp = (k, 0) if p == 1 else (k - 1, 1)
                for s in range(STEPS):
                    copy_products(t, p, s, not mlp)
                    if s == 0 and mlp:
                        drain_z(t - 1, 1 - p, 1)
                    if mlp and s - 1 in MLP_AT:
                        mlp_drain(MLP_AT[s - 1], bk, bp, again)
                drain_z(t, p, 0)
                if mlp:
                    mlp_drain(MLP_AT[STEPS - 1], bk, bp, again)

            tile(0, 0, False)
            tile(0, 1, True)
            tile(1, 0, True)
            with act.Fori(1, NT // 2 - 1) as k:
                tile(k, 1, True, True)
                tile(k + 1, 0, True, True)
            tile(NT // 2 - 1, 1, True, True)
            drain_z(NT - 1, 1, 1)
            for what in MLP_AT.values():
                mlp_drain(what, NT // 2 - 1, 1, True)
            for p in range(2):
                act.wait_ge(y_stored[p], 16 * NT // 2)

        @block.tensor
        def _(pe):
            mm = nc.tensor.matmul
            pe.wait_ge(setup_dve, 2)
            for z in range(2):
                last = nc.tensor.transpose(z_ps[0][:, P * z:P * (z + 1)],
                                           w_diag[:, z].rearrange("p a b -> p (a b)"), ident)
            last.then_inc(setup_pe, 1)
            pe.wait_ge(setup_dve, 4)
            for z in range(2):
                for g in range(G):
                    for side in range(2):
                        last = mm(shared_flat(z)[:, 8 * R * g:8 * R * (g + 1)],
                                  alpha_cut[:, side, g, 8 * z:8 * (z + 1)].rearrange("p k d -> p (k d)"),
                                  slot[:, g, side], start=side == 0, stop=side == 1)
                last.then_inc(shared_full, 1)
            pe.wait_ge(setup_act, 2)
            pe.wait_ge(shared_drained, 2)
            for z in range(2):
                for chunk in (CHUNK_A, CHUNK_B):
                    at = 2 * P * chunk + P * z
                    mm(z_ps[0][:, at:at + P], alpha_slot[:, z, P * chunk:P * (chunk + 1)], whv_diag[:, z],
                       start=True, stop=True)
                for odd in range(2):
                    last = mm(z_ps[1][64 * odd:64 * (odd + 1), P * z:P * (z + 1)], alpha_slot[:, z, 2 * P:2 * P + 64],
                              whv_diag[:, z], start=True, stop=True, tile_position=(0, 64 * odd))
            last.then_inc(setup_pe, 1)
            for c in range(NT * BT):
                at = P * (c % (4 * BT))
                last = nc.tensor.transpose(turned[c // (4 * BT)][0:D].rearrange("p q n -> p (q n)")[:, at:at + P],
                                           dense_in[:, c], ident)
            last.then_inc(setup_pe, 1)

            def turn(k, p, s, first):
                t = 2 * k + p
                n = STEPS * t + s
                zt, chunk, odd = KINDS[s]
                if chunk != KINDS[s - 1][1]:
                    pe.wait_ge(prod_ready, PRODS * t + BT * (chunk + 1))
                if not first or s >= 2:
                    pe.wait_ge(copied, n - 1)
                for q in range(QUADS):
                    h = HALF * zt + 2 * q
                    for c in range(BT):
                        if chunk == CHUNK_C:
                            slots = prod_c[:, p, c, h:h + 2].rearrange("p h j -> p (h j)")
                        else:
                            slots = prod_ab[:, p, chunk, c, h + odd]
                        last = nc.tensor.transpose(turned[s % 2][:, q, P * c:P * (c + 1)], slots, ident)
                last.then_inc(turned_full, 1)

            def contract(k, p, s, first):
                t = 2 * k + p
                n = STEPS * t + s
                zt, chunk, odd = KINDS[s]
                pe.wait_ge(copied, n + 1)
                if s in (0, 2) and not first:
                    pe.wait_ge(z_drained, 2 * (t - 1) + zt + 1)
                for q in range(QUADS):
                    h = HALF * zt + 2 * q
                    weights = m_c[:, h // 2] if chunk == CHUNK_C else m_ab[:, chunk, h + odd]
                    last = mm(z_ps[zt][32 * q:32 * (q + 1), 0:TB], weights,
                              prod_t[:, (STEPS * p + s) % NPROD, q],
                              start=s in (0, 2), stop=chunk == CHUNK_C, tile_position=(0, 32 * q))
                last.then_inc(z_step, 1)

            def mlp(what, t, p):
                use = USES * t + 2
                layer, m = what[:2], int((what + " 0").split()[1])
                if layer == "L1":
                    if m == 0:
                        pe.wait_ge(z_drained, 2 * (t + 1))
                    if m % 2 == 0:
                        pe.wait_ge(shared_drained, use + m // 2 - 1)
                    to = shared[m // 2][:, m % 2]
                    cols = slice(P * m, P * (m + 1))
                    mm(to, w1z[:, 0, cols], z_sb[:, p, 0], start=True, stop=False)
                    mm(to, w1z[:, 1, cols], z_sb[:, p, 1], start=False, stop=False)
                    last = mm(to, w1d[:, cols], dense_t[:, t] if isinstance(t, int) else dense_t[:, bass.ds(t, 1)].squeeze(1),
                              start=False, stop=True)
                    if m % 2 == 1:
                        last.then_inc(shared_full, 1)
                elif layer == "L2":
                    if m == 0:
                        pe.wait_ge(shared_drained, use + 2)
                    for i in range(N1 // P):
                        last = mm(shared[0][:, m], w2[:, i, P * m:P * (m + 1)], h1[:, i],
                                  start=i == 0, stop=i == N1 // P - 1)
                    if m == 1:
                        last.then_inc(shared_full, 1)
                else:
                    pe.wait_ge(shared_drained, use + 3)
                    n = TB // QUADS
                    for i in range(N2 // P):
                        for q in range(QUADS):
                            last = mm(shared[1][32 * q:32 * q + 1, 0, 0:n], w3[:, i:i + 1], h2[:, i, n * q:n * (q + 1)],
                                      start=i == 0, stop=i == N2 // P - 1, tile_position=(0, 32 * q))
                    last.then_inc(shared_full, 1)

            def tile(k, p, before, following):
                t = 2 * k + p
                nk, np_ = (k, 1) if p == 0 else (k + 1, 0)
                for s in range(STEPS):
                    if s + 2 < STEPS:
                        turn(k, p, s + 2, not before)
                    elif following:
                        turn(nk, np_, s + 2 - STEPS, False)
                    contract(k, p, s, not before)
                    if before and s in MLP_AT:
                        mlp(MLP_AT[s], t - 1, 1 - p)

            pe.wait_ge(setup_act, 10)
            turn(0, 0, 0, True)
            turn(0, 0, 1, True)
            pe.wait_ge(weights_loaded, 16 * 21)
            tile(0, 0, False, True)
            with pe.Fori(0, NT // 2 - 1) as k:
                tile(k, 1, True, True)
                tile(k + 1, 0, True, True)
            tile(NT // 2 - 1, 1, True, False)
            for what in MLP_AT.values():
                mlp(what, NT - 1, 1)


_INS = ["dense_ctx", "ids"] + [f"tbl_{i}" for i in range(TABLES)] + [
    "r_x0", "W_top1", "b_top1", "W_top2", "b_top2", "W_top3", "L0_rec_w", "L0_rec_alpha", "L0_rec_hv"]


def kernel(**inputs):
    import numpy as _np
    import concourse.bacc as _bacc
    from concourse import mybir as _mybir
    from concourse.bass_utils import run_bass_kernel_spmd as _run

    nc = _bacc.Bacc("TRN2", target_bir_lowering=False, num_devices=1)
    arrays, args = {}, {}
    for name in _INS:
        a = _np.ascontiguousarray(inputs[name])
        arrays[f"in_{name}"] = a
        args[name] = nc.dram_tensor(f"in_{name}", a.shape, _mybir.dt.from_np(a.dtype), kind="ExternalInput").ap()
    parts, const_at, at = [], {}, 0
    for name, table in constants().items():
        part = table.reshape(P, -1)
        const_at[name] = (at, part.shape[1])
        at += part.shape[1]
        parts.append(part)
    arrays["in_consts"] = _np.concatenate(parts, axis=1)
    consts = nc.dram_tensor("in_consts", arrays["in_consts"].shape, _mybir.dt.float32, kind="ExternalInput").ap()
    out = nc.dram_tensor("out_y", (BATCH, 1), _mybir.dt.float32, kind="ExternalOutput").ap()
    interaction_tower(nc, args["dense_ctx"], args["ids"], [args[f"tbl_{i}"] for i in range(TABLES)], args["r_x0"],
                      args["W_top1"], args["b_top1"], args["W_top2"], args["b_top2"], args["W_top3"],
                      args["L0_rec_w"], args["L0_rec_alpha"], args["L0_rec_hv"], consts, const_at, out)
    r = _run(nc, [arrays], core_ids=[0])
    return r.results[0]["out_y"]
```

```python
from contextlib import ExitStack

import concourse.bass as bass
import numpy as np
from concourse import mybir

F32 = mybir.dt.float32
F32R = mybir.dt.float32r
F16 = mybir.dt.float16
BF16 = mybir.dt.bfloat16
I32 = mybir.dt.int32
ALU = mybir.AluOpType
ACT = mybir.ActivationFunctionType

P = 128
BATCH = 2048
TABLES = 16
F = 39
FP = 40
D = 16
K = 16
H = 16
EMB = TABLES * D
R = 8
FC = P // R
TB = 256
BT = TB // P
NT = BATCH // TB
HALF = 8
QUADS = 4
STEPS = 10
NPROD = 4
N1, N2 = 512, 256
PRODS = 6
USES = 4
CHUNK_A, CHUNK_B, CHUNK_C = range(3)
CHUNKS = [(CHUNK_A, 0, FC), (CHUNK_B, FC, FC), (CHUNK_C, 2 * FC, F - 2 * FC)]
KINDS = [(zt, chunk, odd) for chunk in (CHUNK_A, CHUNK_B) for zt in range(2) for odd in range(2)]
KINDS += [(zt, CHUNK_C, None) for zt in range(2)]
MLP_AT = {0: ("L2 1", 2), 2: ("L3", 2), 3: ("L1 0", 1), 4: ("L1 1", 1), 5: ("L1 2", 1), 6: ("L1 3", 1), 9: ("L2 0", 1)}
LAG = 2
PAIRS = [(13, 14), (1, 15)]
SMALL = [i for pair in PAIRS for i in pair]
GATHERED = [i for i in range(TABLES) if not any(i in pair for pair in PAIRS)]
GATHERS = [[i for i in GATHERED if i <= 6], [i for i in GATHERED if 6 < i <= 13], [i for i in GATHERED if i > 13]]
ROWS = 125
SMALL_CHUNKS = {i: 8 if i in (3, 6, 9, 11) else 10 for i in range(TABLES)}
PARTS = 3
HB = BATCH // 2
ROUNDS = [(half, pair) for half in range(2) for pair in range(len(PAIRS))]
HOTS = [[(i, c) for c in range(SMALL_CHUNKS[PAIRS[pair][0]]) for i in range(2)] for _, pair in ROUNDS]
HOTS_BEFORE = [sum(map(len, HOTS[:r])) for r in range(len(ROUNDS) + 1)]
NHOT = 8
IDS_STEP = 2
TABLES_STEP = IDS_STEP + 2 * PARTS - 1
CUT_STEP = TABLES_STEP + 6
DENSE_STEP = CUT_STEP + 2 * PARTS - 1 + 6
WEIGHTS_STEP = DENSE_STEP + 2 * PARTS - 1 + 5
N_SMALL_LOADS = 6
N_WEIGHT_LOADS = 16 + 6 + 4
DENSE_PARTS = [0, 0, 1, 0, 2, 1]
W_PARTS = [0, 1, 0, 2, 0, 1]


def first_embedding(f):
    first, count, m, step = next(r for r in RUNS if r[0] <= f < r[0] + r[1])
    return m + step * (f - first)


def feature_runs():
    def fits(f, m):
        return 256 * f // F >= m >= 0 and (256 * f + 255) // F < m + R <= EMB
    runs, f = [], 0
    while f < F:
        end = min(F, FC * (f // FC + 1))
        best = (f, 0, 0, 0)
        for step in range(R):
            for m in range(256 * f // F, max(0, 256 * f // F - 2) - 1, -1):
                n = 0
                while f + n < end and fits(f + n, m + step * n):
                    n += 1
                if n > best[1]:
                    best = (f, n, m, step)
        runs.append(best)
        f += best[1]
    return runs


RUNS = feature_runs()


def constants():
    ident = np.eye(P, dtype=np.float32)
    groups = FP // 8
    below = np.zeros((P, groups, D), np.float32)
    above = np.zeros((P, groups, D), np.float32)
    slot = np.zeros((P, groups, 2, 8 * R), np.float32)
    for n in range(16 * F):
        g, row, f = n // P, n % P, n // 16
        low, high = 16 * n // F, (16 * n + 15) // F
        for d in range(D):
            (below if (16 * n + d) // F == low else above)[row, g, d] = 1.0
        for side, m in enumerate((low, high)):
            slot[row, g, side, R * (f % 8) + m - first_embedding(f)] = 1.0
    block = np.kron(np.eye(8, dtype=np.float32), np.ones((H, 1), np.float32))
    rows = {n: np.add.outer(float(n) * np.arange(P), np.arange(n)).astype(np.float32) for n in (8, 10)}
    combine = np.zeros((P, 2 * D), np.float32)
    for i in range(2):
        for part in range(PARTS):
            for d in range(D):
                combine[64 * i + D * part + d, D * i + d] = 1.0
    part_mask = np.zeros((P, PARTS), np.float32)
    for i, part in enumerate(W_PARTS):
        part_mask[D * i:D * (i + 1), part] = 1.0
    return {"rows8": rows[8], "rows10": rows[10], "combine": combine, "part_mask": part_mask, "ident": ident, "below": below, "above": above, "slot": slot, "block": block}


def interaction_tower(nc, dense_ctx, ids, tables, x0, w_top1, b_top1, w_top2, b_top2, w_top3,
                      w, alpha, hv, consts, const_at, out):
    G = FP // 8
    NALPHA = 16 * F
    with ExitStack() as ctx:
        def sb(name, shape, dt=F32):
            return ctx.enter_context(nc.sbuf_tensor(name, shape, dt))

        def bank(name, shape):
            return ctx.enter_context(nc.psum_tensor(name, shape, F32))

        def sem(name):
            return ctx.enter_context(nc.semaphore(name))

        const = sb("const", [P, consts.shape[1]])

        def const_view(name, *dims):
            a, n = const_at[name]
            v = const[:, a:a + n]
            if len(dims) == 2:
                return v.rearrange("p (a b) -> p a b", a=dims[0])
            if len(dims) == 3:
                return v.rearrange("p (a b c) -> p a b c", a=dims[0], b=dims[1])
            return v

        ident = const_view("ident")
        below = const_view("below", G, D)
        above = const_view("above", G, D)
        slot = const_view("slot", G, 2, 8 * R)
        block_mask = const_view("block")
        row_of = {8: const_view("rows8"), 10: const_view("rows10")}
        part_mask = const_view("part_mask")
        ident_b = sb("ident_b", [P, P], BF16)
        ident_h = sb("ident_h", [P, P], F16)
        combine_b = sb("combine_b", [P, 2 * D], BF16)
        w1z_hi = sb("w1z_hi", [P, 2, N1], F32R)
        w1z_lo = sb("w1z_lo", [P, 2, N1], F32R)
        w2_hi = sb("w2_hi", [P, N1 // P, N2], F32R)
        w2_lo = sb("w2_lo", [P, N1 // P, N2], F32R)
        w1d = sb("w1d", [len(W_PARTS) * D, N1])
        w1d_six = sb("w1d_six", [len(W_PARTS) * D, N1], BF16)
        w3_in = sb("w3_in", [P, N2 // P])
        w3 = sb("w3", [P, N2 // P, 32])
        b1 = sb("b1", [P, N1 // P])
        b2 = sb("b2", [P, N2 // P])
        hv_col = sb("hv_col", [P, 2])
        w_rows = sb("w_rows", [P, 2, D])
        alpha_rows = sb("alpha_rows", [P, G, K])
        whv_diag = sb("whv_diag", [P, 2, P])
        alpha_slot = sb("alpha_slot", [P, 2, FP * R])
        m_ab = sb("m_ab", [P, 2, H, 32])
        m_c = sb("m_c", [P, H // 2, 32])
        dense_in = sb("dense_in", [P, NT * BT, D])
        dense_part = sb("dense_part", [P, PARTS, NT * BT, D], BF16)
        dense_six = sb("dense_six", [P, NT * BT, len(DENSE_PARTS), D], BF16)
        dense_t = sb("dense_t", [len(DENSE_PARTS) * D, NT, TB], BF16)
        first_chunk = {}
        for i in SMALL:
            first_chunk[i] = sum(SMALL_CHUNKS[j] for j in SMALL[:SMALL.index(i)])
        n_chunks = sum(SMALL_CHUNKS[i] for i in SMALL)
        ids_all = sb("ids_all", [P, NT * BT, TABLES], I32)
        ids_h = sb("ids_h", [P, NT * BT, TABLES], F16)
        small = sb("small", [ROWS, n_chunks, D])
        small_parts = sb("small_parts", [ROWS, n_chunks, 4, D], BF16)
        x_in = sb("x_in", [P, 2, BT, F * H])
        emb = sb("emb", [P, NT * BT, EMB])
        emb_slot = sb("emb_slot", [P, 2, BT, FP * R])
        prod_ab = sb("prod_ab", [P, 2, 2, BT, H, P])
        prod_c = sb("prod_c", [P, 2, BT, H, P // 2])
        prod_t = sb("prod_t", [P, NPROD, QUADS, TB])

        def words(p, chunk, at, n):
            return prod_ab[:, p, chunk].rearrange("p c h j -> p (c h j)")[:, at:at + n]

        ids_b = words(0, 0, 0, 2 * HB).bitcast(F16).rearrange("p (r i n) -> p r i n", r=2, i=2)
        small_rest = words(0, 0, 2 * HB, 2 * n_chunks * D)[0:ROWS].rearrange("p (j c d) -> p j c d", j=2, d=D)
        n_cut = 2 * G * K * D
        alpha_cut = words(0, 1, 0, n_cut).rearrange("p (i g k d) -> p i g k d", i=2, g=G, k=K)
        w_diag = words(0, 1, n_cut, 2 * P).rearrange("p (z a b) -> p z a b", z=2, a=8)
        looked_t = words(0, 1, n_cut + 2 * P, HB).bitcast(BF16).rearrange("p (i n) -> p i n", i=2)
        hot = words(1, 0, 0, NHOT * HB // 2).bitcast(BF16).rearrange("p (i n) -> p i n", n=HB)
        w1d_part = words(1, 0, 0, PARTS * N1 // 2)[0:len(W_PARTS) * D].bitcast(BF16).rearrange("p (j n) -> p j n", j=PARTS)
        dense_rest = words(1, 0, 1024, 2 * NT * BT * D).rearrange("p (j c d) -> p j c d", j=2, d=D)
        w1z = words(1, 1, 0, 2 * N1).rearrange("p (z n) -> p z n", z=2)
        w2 = words(1, 1, 2 * N1, N1 // P * N2).rearrange("p (m n) -> p m n", n=N2)
        w1d_rest = words(1, 1, 2048, 2 * N1)[0:len(W_PARTS) * D].rearrange("p (j n) -> p j n", j=2)
        w1d_sum = words(1, 1, 3072, 2 * N1)[0:len(W_PARTS) * D].rearrange("p (j n) -> p j n", j=2)
        z_sb = sb("z_sb", [P, 2, 2, TB])
        z_hi = sb("z_hi", [P, 2, 2, TB], F32R)
        z_lo = sb("z_lo", [P, 2, 2, TB], F32R)
        h1 = sb("h1", [P, N1 // P, TB])
        h1_hi = sb("h1_hi", [P, N1 // P, TB], F32R)
        h1_lo = sb("h1_lo", [P, N1 // P, TB], F32R)
        h2 = sb("h2", [P, N2 // P, TB])
        y = sb("y", [P, NT, TB // QUADS])

        turned = [bank(f"turned{i}", [P, QUADS, TB]) for i in range(2)]
        z_banks = bank("z_banks", [P, 2, 512])
        z_ps = [z_banks[:, i] for i in range(2)]
        shared = [bank(f"shared{i}", [P, 2, TB]) for i in range(2)]

        small_loaded = sem("small_loaded")
        const_loaded = sem("const_loaded")
        weights_loaded = sem("weights_loaded")
        x_loaded = [sem(f"x_loaded{i}") for i in range(2)]
        gathered = [[sem(f"gathered{i}_{c}") for c in range(3)] for i in range(2)]
        tables_loaded = sem("tables_loaded")
        ids_here = sem("ids_here")
        split = sem("split")
        split_act = sem("split_act")
        spread = sem("spread")
        spread_copied = sem("spread_copied")
        hot_ready = sem("hot_ready")
        hot_used = sem("hot_used")
        looked_copied = sem("looked_copied")
        turned_back = sem("turned_back")
        looked_ready = sem("looked_ready")
        dense_turned = sem("dense_turned")
        dense_copied = sem("dense_copied")
        lo_ready = sem("lo_ready")
        cleared = sem("cleared")
        setup_pe = sem("setup_pe")
        setup_act = sem("setup_act")
        slotted = sem("slotted")
        prod_ready = sem("prod_ready")
        turned_full = sem("turned_full")
        copied = sem("copied")
        z_step = sem("z_step")
        z_drained = sem("z_drained")
        shared_full = sem("shared_full")
        shared_drained = sem("shared_drained")
        y_stored = sem("y_stored")

        out_rows = out.rearrange("(t q n) o -> q t (n o)", t=NT, q=QUADS)
        x_rows = x0.rearrange("(t c p) f h -> t p c (f h)", c=BT, p=P)
        dense_rows = dense_ctx.rearrange("(c p) s -> p c s", p=P)
        w1_rows = w_top1[0:K * H, :].rearrange("(k z hh) n -> z hh k n", z=2, hh=HALF)

        block = ctx.enter_context(nc.Block())

        def windows(values, m, count, step):
            (pstep, pn), (cstep, cn), _ = values.ap
            return bass.AP(values.tensor, values.offset + m, [[pstep, pn], [cstep, cn], [step, count], [1, R]])

        def at_tile(rows, t):
            if isinstance(t, int):
                return rows[t]
            return rows[bass.ds(t, 1)].squeeze(0)

        def flat(tile):
            return tile[:].rearrange("p a b -> p (a b)")

        @block.sync
        def _(sp):
            def load(k, p, again):
                t = 2 * k + p
                if again:
                    sp.wait_ge(prod_ready, PRODS * (t - 1))
                sp.dma_start(x_in[:, p], at_tile(x_rows, t)).then_inc(x_loaded[p], 16)

            sp.dma_start(ids_all[:], ids.rearrange("(c p) s -> p c s", p=P)).then_inc(ids_here, 16)
            for i in SMALL:
                at = first_chunk[i]
                sp.dma_start(small[:, at:at + SMALL_CHUNKS[i]],
                             tables[i].rearrange("(p c) d -> p c d", p=ROWS)).then_inc(tables_loaded, 16)
            with nc.allow_non_contiguous_dma(reason="small vectors, one element to a partition"):
                sp.wait_ge(cleared, 1)
                sp.dma_start(alpha_rows[:, 0:NALPHA // P],
                              alpha[0:P * (NALPHA // P), :].rearrange("(g p) k -> p g k", p=P)).then_inc(small_loaded, 16)
                sp.dma_start(alpha_rows[0:NALPHA % P, NALPHA // P],
                              alpha[P * (NALPHA // P):NALPHA, :]).then_inc(small_loaded, 16)
                sp.dma_start(w_rows[:], w.rearrange("(z k) h d -> z (k h) d", z=2).rearrange("z q d -> q z d")).then_inc(small_loaded, 16)
                sp.dma_start(dense_in[:], dense_rows).then_inc(small_loaded, 16)
                hv_rows = hv.rearrange("(z k) d o -> z (k d) o", z=2)
                for z in range(2):
                    sp.dma_start(hv_col[:, z:z + 1], hv_rows[z]).then_inc(small_loaded, 16)
            load(0, 0, False)
            load(0, 1, False)
            with nc.allow_non_contiguous_dma(reason="small vectors, one element to a partition"):
                for z in range(2):
                    for hh in range(HALF):
                        sp.dma_start(w1z[K * hh:K * (hh + 1), z], w1_rows[z, hh]).then_inc(weights_loaded, 16)
                for i in range(len(W_PARTS)):
                    sp.dma_start(w1d[D * i:D * (i + 1)], w_top1[K * H:K * H + D, :]).then_inc(weights_loaded, 16)
                sp.dma_start(w2, w_top2.rearrange("(m p) n -> p m n", p=P)).then_inc(weights_loaded, 16)
                sp.dma_start(w3_in[:], w_top3.rearrange("(m p) o -> p (m o)", p=P)).then_inc(weights_loaded, 16)
                sp.dma_start(b1[:], b_top1.rearrange("(m p) -> p m", p=P)).then_inc(weights_loaded, 16)
                sp.dma_start(b2[:], b_top2.rearrange("(m p) -> p m", p=P)).then_inc(weights_loaded, 16)
            with sp.Fori(1, NT // 2) as k:
                load(k, 0, True)
                load(k, 1, True)

        @block.gpsimd
        def _(pool):
            pool.wait_ge(ids_here, 16)
            for t in range(NT):
                k, p = divmod(t, 2)
                for chunk in range(3):
                    if k and GATHERS[chunk]:
                        pool.wait_ge(gathered[p][chunk], 16 * len(GATHERS[chunk]) * BT * k)
                    for s in GATHERS[chunk]:
                        for c in range(BT * t, BT * (t + 1)):
                            pool.indirect_dma_start(
                                emb[:, c, D * s:D * (s + 1)], None, tables[s],
                                bass.IndirectOffsetOnAxis(ids_all[:, c, s:s + 1], 0)).then_inc(gathered[p][chunk], 16)

        @block.vector
        def _(dve):
            done = [0]

            def step(instruction):
                done[0] += 1
                instruction.then_inc(split, 1)
                dve.wait_ge(split, done[0])

            def three_parts(source, rest, part):
                for i in range(PARTS):
                    step(nc.vector.tensor_copy(part(i), source))
                    if i < PARTS - 1:
                        step(nc.vector.tensor_tensor(rest(i), source, part(i), ALU.subtract))
                        source = rest(i)

            nc.vector.memset(alpha_rows[:], 0.0).then_inc(cleared, 1)
            nc.vector.memset(small_parts[:], 0.0).then_inc(cleared, 1)
            dve.wait_ge(const_loaded, 16)
            step(nc.vector.tensor_copy(ident_h[:], ident))
            dve.wait_ge(ids_here, 16)
            step(nc.vector.tensor_copy(ids_h[:], ids_all[:]))
            assert done[0] == IDS_STEP
            dve.wait_ge(cleared, 2)
            dve.wait_ge(tables_loaded, 16 * len(SMALL))
            three_parts(small[:], lambda j: small_rest[:, j], lambda j: small_parts[:, :, j])
            assert done[0] == TABLES_STEP

            def one_hots(r):
                pair = ROUNDS[r][1]
                for at, (i, chunk) in enumerate(HOTS[r]):
                    n = HOTS_BEFORE[r] + at
                    if chunk == 0:
                        dve.wait_ge(spread_copied, 2 * r + i + 1)
                    if n >= NHOT:
                        dve.wait_ge(hot_used, n - NHOT + 1)
                    nc.vector.tensor_scalar(hot[0:ROWS, n % NHOT], ids_b[0:ROWS, r % 2, i],
                                            row_of[SMALL_CHUNKS[PAIRS[pair][i]]][0:ROWS, chunk:chunk + 1], None,
                                            ALU.is_equal).then_inc(hot_ready, 1)

            one_hots(0)
            step(nc.vector.tensor_copy(ident_b[:], ident))
            step(nc.vector.tensor_copy(combine_b[:], const_view("combine")))
            dve.wait_ge(small_loaded, 16 * N_SMALL_LOADS)
            for z in range(2):
                step(nc.vector.tensor_tensor(
                    w_diag[:, z], w_rows[:, z].unsqueeze(1).broadcast_to([P, 8, D]),
                    block_mask.unsqueeze(2).broadcast_to([P, 8, D]), ALU.mult))
            for side, mask in enumerate((below, above)):
                step(nc.vector.tensor_tensor(
                    alpha_cut[:, side], alpha_rows[:].unsqueeze(3).broadcast_to([P, G, K, D]),
                    mask.unsqueeze(2).broadcast_to([P, G, K, D]), ALU.mult))
            assert done[0] == CUT_STEP
            nc.vector.memset(m_ab[:], 0.0).then_inc(cleared, 1)
            nc.vector.memset(m_c[:], 0.0).then_inc(cleared, 1)
            nc.vector.memset(w3[:], 0.0).then_inc(cleared, 1)
            nc.vector.memset(prod_c[:, :, :, :, R * CHUNKS[CHUNK_C][2]:], 0.0).then_inc(cleared, 1)
            for r in range(1, len(ROUNDS)):
                one_hots(r)

            def split_weights():
                three_parts(dense_in[:], lambda j: dense_rest[:, j], lambda j: dense_part[:, j])
                for i, part in enumerate(DENSE_PARTS):
                    step(nc.vector.tensor_copy(dense_six[:, :, i], dense_part[:, part]))
                assert done[0] == DENSE_STEP
                dve.wait_ge(weights_loaded, 16 * N_WEIGHT_LOADS)
                three_parts(w1d[:], lambda j: w1d_rest[:, j], lambda j: w1d_part[:, j])
                mask = part_mask[0:len(W_PARTS) * D]
                step(nc.vector.tensor_scalar(w1d_sum[:, 0], w1d_part[:, 0], mask[:, 0:1], None, ALU.mult))
                step(nc.vector.scalar_tensor_tensor(w1d_sum[:, 1], w1d_part[:, 1], mask[:, 1:2], w1d_sum[:, 0],
                                                    ALU.mult, ALU.add))
                step(nc.vector.scalar_tensor_tensor(w1d_six[:], w1d_part[:, 2], mask[:, 2:3], w1d_sum[:, 1],
                                                    ALU.mult, ALU.add))
                dve.wait_ge(split_act, 3)
                step(nc.vector.tensor_tensor(w1z_lo[:], w1z, w1z_hi[:].bitcast(F32), ALU.subtract))
                step(nc.vector.tensor_tensor(w2_lo[:], w2, w2_hi[:].bitcast(F32), ALU.subtract))
                assert done[0] == WEIGHTS_STEP

            def z_low(k, p):
                t = 2 * k + p
                dve.wait_ge(z_drained, 2 * (t + 1))
                nc.vector.tensor_tensor(z_lo[:, p], z_sb[:, p], z_hi[:, p].bitcast(F32),
                                        ALU.subtract).then_inc(lo_ready, 1)

            def h1_low(t, i):
                dve.wait_ge(shared_drained, USES * t + 3 + i)
                part = slice(2 * i, 2 * i + 2)
                nc.vector.tensor_tensor(h1_lo[:, part], h1[:, part], h1_hi[:, part].bitcast(F32),
                                        ALU.subtract).then_inc(lo_ready, 1)

            def products(k, p, again):
                t = 2 * k + p
                if again:
                    dve.wait_ge(prod_ready, PRODS * (t - 1))
                embeddings = emb[:, BT * t:BT * (t + 1)] if isinstance(t, int) else emb[:, bass.ds(BT * t, BT)]
                slots_done = 0
                for chunk, feature, count in CHUNKS:
                    if GATHERS[chunk]:
                        dve.wait_ge(gathered[p][chunk], 16 * len(GATHERS[chunk]) * BT * (k + 1))
                    for f, n, m, stride in RUNS:
                        if feature <= f < feature + count:
                            nc.vector.tensor_copy(
                                emb_slot[:, p, :, R * f:R * (f + n)].rearrange("p c (f r) -> p c f r", r=R),
                                windows(embeddings, m, n, stride)).then_inc(slotted, 1)
                            slots_done += 1
                    if chunk == CHUNK_A:
                        dve.wait_ge(x_loaded[p], 16 * (k + 1))
                    dve.wait_ge(slotted, len(RUNS) * t + slots_done)
                    if again:
                        dve.wait_ge(turned_full, STEPS * (t - 2) + min(STEPS, 4 * (chunk + 1)))
                    for c in range(BT):
                        to = prod_c[:, p, c, :, 0:R * count] if chunk == CHUNK_C else prod_ab[:, p, chunk, c]
                        rows = x_in[:, p, c].rearrange("p (f h) -> p h f", h=H)[:, :, feature:feature + count]
                        slots = emb_slot[:, p, c, R * feature:R * (feature + count)]
                        nc.vector.tensor_tensor(
                            to.rearrange("p h (f r) -> p h f r", r=R),
                            rows.unsqueeze(3).broadcast_to([P, H, count, R]),
                            slots.unsqueeze(1).broadcast_to([P, H, R * count]).rearrange("p h (f r) -> p h f r", r=R),
                            ALU.mult).then_inc(prod_ready, 1)
                    if again:
                        if chunk == CHUNK_A:
                            z_low(k - 1, p)
                        else:
                            h1_low(t - 2, chunk - 1)

            dve.wait_ge(setup_act, 8)
            dve.wait_ge(looked_ready, len(ROUNDS))
            products(0, 0, False)
            dve.wait_ge(hot_used, HOTS_BEFORE[-1])
            split_weights()
            products(0, 1, False)
            with dve.Fori(1, NT // 2) as k:
                products(k, 0, True)
                products(k, 1, True)
            for p in range(2):
                z_low(NT // 2 - 1, p)
                for i in range(2):
                    h1_low(NT - 2 + p, i)

        @block.scalar
        def _(act):
            act.dma_start(const[:], consts).then_inc(const_loaded, 16)

            def copy_spread(r):
                for i in range(2):
                    act.wait_ge(spread, 2 * r + i + 1)
                    if r >= 2:
                        act.wait_ge(hot_ready, HOTS_BEFORE[r - 1])
                    nc.scalar.activation(ids_b[:, r % 2, i], flat(turned[i]), ACT.Copy).then_inc(spread_copied, 1)

            def copy_looked(r):
                act.wait_ge(hot_used, HOTS_BEFORE[r + 1])
                nc.scalar.activation(looked_t[:, r % 2], flat(z_banks), ACT.Copy).then_inc(looked_copied, 1)

            def keep_looked(r):
                half, pair = ROUNDS[r]
                act.wait_ge(turned_back, r + 1)
                n = HB // P
                first, second = PAIRS[pair]
                to = emb[:, n * half:n * (half + 1)].rearrange("p c (s d) -> p c s d", d=D)
                nc.scalar.activation(
                    to[:, :, first:second + 1:second - first],
                    shared[r % 2][:, 0].rearrange("p (c i d) -> p c i d", i=2, d=D), ACT.Copy).then_inc(looked_ready, 1)

            def m_setup():
                act.wait_ge(setup_pe, 1)
                act.wait_ge(small_loaded, 16 * N_SMALL_LOADS)
                for z in range(2):
                    nc.scalar.activation(whv_diag[:, z], flat(shared[z])[:, 384:512], ACT.Copy,
                                         scale=hv_col[:, z:z + 1]).then_inc(setup_act, 1)
                act.wait_ge(shared_full, 2)
                for z in range(2):
                    nc.scalar.activation(alpha_slot[:, z], flat(shared[z])[:, 0:FP * R], ACT.Copy).then_inc(shared_drained, 1)
                act.wait_ge(setup_pe, 2)
                act.wait_ge(cleared, 4)
                m_view = [shared[0][:, 0], shared[0][:, 1], shared[1][:, 0]]
                for odd in range(2):
                    cols = slice(K * odd, K * (odd + 1))
                    for chunk in (CHUNK_A, CHUNK_B):
                        nc.scalar.activation(
                            m_ab[:, chunk, odd::2, cols],
                            m_view[chunk].rearrange("p (k h) -> p h k", h=H)[:, odd::2, :], ACT.Copy).then_inc(setup_act, 1)
                    rows = slice(64 * odd, 64 * (odd + 1))
                    nc.scalar.activation(
                        m_c[rows, :, cols],
                        m_view[CHUNK_C].rearrange("p (k h) -> p h k", h=H)[rows, odd::2, :], ACT.Copy).then_inc(setup_act, 1)

            copy_spread(0)
            for r in range(len(ROUNDS)):
                if r + 1 < len(ROUNDS):
                    copy_spread(r + 1)
                copy_looked(r)
                if r == 0:
                    m_setup()
                else:
                    keep_looked(r - 1)
            keep_looked(len(ROUNDS) - 1)
            act.wait_ge(cleared, 6)
            act.wait_ge(weights_loaded, 16 * N_WEIGHT_LOADS)
            nc.scalar.activation(w3[:, :, 0], w3_in[:], ACT.Copy).then_inc(split_act, 1)
            act.wait_ge(weights_loaded, 16 * N_WEIGHT_LOADS)
            nc.scalar.activation(w1z_hi[:], w1z, ACT.Copy).then_inc(split_act, 1)
            nc.scalar.activation(w2_hi[:], w2, ACT.Copy).then_inc(split_act, 1)

            def copy_products(t, p, s, again):
                n = STEPS * t + s
                act.wait_ge(turned_full, n + 1)
                if again or s >= NPROD:
                    act.wait_ge(z_step, n - NPROD + 1)
                nc.scalar.activation(prod_t[:, (STEPS * p + s) % NPROD], turned[s % 2][:], ACT.Copy).then_inc(copied, 1)

            def drain_z(t, p, zt):
                act.wait_ge(z_step, STEPS * t + STEPS - 1 + zt)
                nc.scalar.activation(z_sb[:, p, zt], z_ps[zt][:, 0:TB], ACT.Copy)
                nc.scalar.activation(z_hi[:, p, zt], z_ps[zt][:, 0:TB], ACT.Copy).then_inc(z_drained, 1)

            def mlp_drain(what, t):
                use = USES * t + 2
                if what in ("L1 1", "L1 3"):
                    m = int(what[3]) - 1
                    source = shared[m // 2]
                    act.wait_ge(shared_full, use + m // 2 + 1)
                    for i in range(2):
                        for to in (h1, h1_hi):
                            last = nc.scalar.activation(to[:, m + i], source[:, i], ACT.Relu, bias=b1[:, m + i:m + i + 1])
                    last.then_inc(shared_drained, 1)
                elif what == "L2 1":
                    act.wait_ge(shared_full, use + 3)
                    for i in range(2):
                        last = nc.scalar.activation(h2[:, i], shared[0][:, i], ACT.Relu, bias=b2[:, i:i + 1])
                    last.then_inc(shared_drained, 1)
                elif what == "L3":
                    act.wait_ge(shared_full, use + 4)
                    to = y[:, t] if isinstance(t, int) else y[:, bass.ds(t, 1)].squeeze(1)
                    nc.scalar.activation(to, shared[1][:, 0, 0:TB // QUADS], ACT.Copy).then_inc(shared_drained, 1)

            def tile(k, p, earlier):
                t = 2 * k + p
                for s in range(STEPS):
                    copy_products(t, p, s, earlier)
                    if s < 2 and earlier:
                        drain_z(t - 1, 1 - p, s)
                    if s - LAG in MLP_AT:
                        what, back = MLP_AT[s - LAG]
                        if back <= earlier:
                            mlp_drain(what, t - back)

            tile(0, 0, 0)
            for i in range(2):
                act.wait_ge(dense_turned, i + 1)
                nc.scalar.activation(dense_t[:].rearrange("p t n -> p (t n)")[:, 4 * TB * i:4 * TB * (i + 1)],
                                     flat(shared[i])[0:len(DENSE_PARTS) * D].bitcast(BF16), ACT.Copy).then_inc(dense_copied, 1)
            tile(0, 1, 1)
            with act.Fori(1, NT // 2 - 1) as k:
                tile(k, 0, 2)
                tile(k, 1, 2)
            tile(NT // 2 - 1, 0, 2)
            tile(NT // 2 - 1, 1, 2)
            for zt in range(2):
                drain_z(NT - 1, 1, zt)
            for t in (NT, NT + 1):
                for what, back in MLP_AT.values():
                    if t - back < NT:
                        mlp_drain(what, t - back)
            act.wait_ge(shared_drained, USES * NT + 2)
            for q in range(QUADS):
                act.dma_start(out_rows[q:q + 1], y[32 * q:32 * q + 1]).then_inc(y_stored, 16)
            act.wait_ge(y_stored, 16 * QUADS)

        @block.tensor
        def _(pe):
            mm = nc.tensor.matmul

            def spread_ids(r):
                half, pair = ROUNDS[r]
                for i, s in enumerate(PAIRS[pair]):
                    if r:
                        pe.wait_ge(spread_copied, 2 * (r - 1) + i + 1)
                    for c in range(HB // P):
                        last = mm(flat(turned[i])[:, P * c:P * (c + 1)],
                                  ids_h[:, HB // P * half + c, s:s + 1].broadcast_to([P, P]), ident_h[:],
                                  start=True, stop=True)
                    last.then_inc(spread, 1)

            def look_up(r):
                pair = ROUNDS[r][1]
                if r:
                    pe.wait_ge(looked_copied, r)
                chunks = SMALL_CHUNKS[PAIRS[pair][0]]
                for chunk in range(chunks):
                    n = HOTS_BEFORE[r] + 2 * chunk
                    pe.wait_ge(hot_ready, n + 2)
                    for half in range(2):
                        for i in range(2):
                            at = first_chunk[PAIRS[pair][i]] + chunk
                            last = mm(z_ps[half][64 * i:64 * (i + 1), :],
                                      small_parts[:, at].rearrange("p j d -> p (j d)"),
                                      hot[0:ROWS, (n + i) % NHOT, 512 * half:512 * (half + 1)],
                                      start=chunk == 0, stop=chunk == chunks - 1, tile_position=(0, 64 * i))
                            if half:
                                last.then_inc(hot_used, 1)

            def turn_back(r):
                pe.wait_ge(looked_copied, r + 1)
                if r >= 2:
                    pe.wait_ge(looked_ready, r - 1)
                for c in range(HB // P):
                    last = mm(shared[r % 2][:, 0, 2 * D * c:2 * D * (c + 1)], looked_t[:, r % 2, P * c:P * (c + 1)],
                              combine_b[:], start=True, stop=True)
                last.then_inc(turned_back, 1)

            def m_setup():
                pe.wait_ge(split, CUT_STEP - 2)
                for z in range(2):
                    last = nc.tensor.transpose(flat(shared[z])[:, 384:512], w_diag[:, z].rearrange("p a b -> p (a b)"), ident)
                last.then_inc(setup_pe, 1)
                pe.wait_ge(setup_act, 2)
                pe.wait_ge(split, CUT_STEP)
                for z in range(2):
                    for g in range(G):
                        for side in range(2):
                            last = mm(flat(shared[z])[:, 8 * R * g:8 * R * (g + 1)],
                                      alpha_cut[:, side, g, 8 * z:8 * (z + 1)].rearrange("p k d -> p (k d)"),
                                      slot[:, g, side], start=side == 0, stop=side == 1)
                    last.then_inc(shared_full, 1)
                pe.wait_ge(shared_drained, 2)
                for z in range(2):
                    for chunk in (CHUNK_A, CHUNK_B):
                        mm(shared[0][:, chunk, P * z:P * (z + 1)], alpha_slot[:, z, P * chunk:P * (chunk + 1)], whv_diag[:, z],
                           start=True, stop=True)
                    for odd in range(2):
                        last = mm(shared[1][64 * odd:64 * (odd + 1), 0, P * z:P * (z + 1)], alpha_slot[:, z, 2 * P:2 * P + 64],
                                  whv_diag[:, z], start=True, stop=True, tile_position=(0, 64 * odd))
                last.then_inc(setup_pe, 1)

            def turn_dense():
                pe.wait_ge(split, DENSE_STEP)
                for i in range(2):
                    for c in range(NT * BT // 2):
                        last = nc.tensor.transpose(flat(shared[i])[0:len(DENSE_PARTS) * D].bitcast(BF16)[:, P * c:P * (c + 1)],
                                                   dense_six[:, NT * BT // 2 * i + c].rearrange("p j d -> p (j d)"), ident_b[:])
                    last.then_inc(dense_turned, 1)

            def turn(k, p, s, first):
                t = 2 * k + p
                n = STEPS * t + s
                zt, chunk, odd = KINDS[s]
                if chunk != KINDS[s - 1][1]:
                    pe.wait_ge(prod_ready, PRODS * t + BT * (chunk + 1))
                if not first or s >= 2:
                    pe.wait_ge(copied, n - 1)
                for q in range(QUADS):
                    h = HALF * zt + 2 * q
                    for c in range(BT):
                        if chunk == CHUNK_C:
                            slots = prod_c[:, p, c, h:h + 2].rearrange("p h j -> p (h j)")
                        else:
                            slots = prod_ab[:, p, chunk, c, h + odd]
                        last = nc.tensor.transpose(turned[s % 2][:, q, P * c:P * (c + 1)], slots, ident)
                last.then_inc(turned_full, 1)

            def contract(k, p, s, first):
                t = 2 * k + p
                n = STEPS * t + s
                zt, chunk, odd = KINDS[s]
                pe.wait_ge(copied, n + 1)
                if s in (0, 2) and not first:
                    pe.wait_ge(z_drained, 2 * (t - 1) + zt + 1)
                for q in range(QUADS):
                    h = HALF * zt + 2 * q
                    weights = m_c[:, h // 2] if chunk == CHUNK_C else m_ab[:, chunk, h + odd]
                    last = mm(z_ps[zt][32 * q:32 * (q + 1), 0:TB], weights,
                              prod_t[:, (STEPS * p + s) % NPROD, q],
                              start=s in (0, 2), stop=chunk == CHUNK_C, tile_position=(0, 32 * q))
                last.then_inc(z_step, 1)

            def mlp(what, t, p):
                use = USES * t + 2
                layer, m = what[:2], int((what + " 0").split()[1])
                cols = slice(P * m, P * (m + 1))
                if layer == "L1":
                    if m == 0:
                        pe.wait_ge(lo_ready, 3 * t + 1)
                    if m % 2 == 0:
                        pe.wait_ge(shared_drained, use + m // 2 - 1)
                    to = shared[m // 2][:, m % 2]
                    mm(to, w1d_six[:, cols], dense_t[:, t] if isinstance(t, int) else dense_t[:, bass.ds(t, 1)].squeeze(1),
                       start=True, stop=False)
                    for n, (weights, z) in enumerate([(w1z_hi, z_hi), (w1z_lo, z_hi), (w1z_hi, z_lo)]):
                        for zt in range(2):
                            last = mm(to, weights[:, zt, cols], z[:, p, zt], start=False, stop=n == 2 and zt == 1)
                    if m % 2 == 1:
                        last.then_inc(shared_full, 1)
                elif layer == "L2":
                    if m == 0:
                        pe.wait_ge(lo_ready, 3 * t + 3)
                    for n, (weights, h) in enumerate([(w2_hi, h1_hi), (w2_lo, h1_hi), (w2_hi, h1_lo)]):
                        for i in range(N1 // P):
                            last = mm(shared[0][:, m], weights[:, i, cols], h[:, i],
                                      start=n == 0 and i == 0, stop=n == 2 and i == N1 // P - 1)
                    if m == 1:
                        last.then_inc(shared_full, 1)
                else:
                    pe.wait_ge(shared_drained, use + 3)
                    n = TB // QUADS
                    for i in range(N2 // P):
                        for q in range(QUADS):
                            last = mm(shared[1][32 * q:32 * (q + 1), 0, 0:n], w3[:, i], h2[:, i, n * q:n * (q + 1)],
                                      start=i == 0, stop=i == N2 // P - 1, tile_position=(0, 32 * q))
                    last.then_inc(shared_full, 1)

            def tile(k, p, earlier, following):
                t = 2 * k + p
                nk, np_ = (k, 1) if p == 0 else (k + 1, 0)
                for s in range(STEPS):
                    if s + 2 < STEPS:
                        turn(k, p, s + 2, not earlier)
                    elif following:
                        turn(nk, np_, s + 2 - STEPS, False)
                    contract(k, p, s, not earlier)
                    if s in MLP_AT:
                        what, back = MLP_AT[s]
                        if back <= earlier:
                            mlp(what, t - back, (p + back) % 2)

            pe.wait_ge(split, IDS_STEP)
            spread_ids(0)
            pe.wait_ge(split, TABLES_STEP)
            for r in range(len(ROUNDS)):
                if r + 1 < len(ROUNDS):
                    spread_ids(r + 1)
                look_up(r)
                if r == 0:
                    m_setup()
                else:
                    if r == 1:
                        pe.wait_ge(setup_act, 8)
                    turn_back(r - 1)
            turn_back(len(ROUNDS) - 1)
            pe.wait_ge(spread_copied, 2 * len(ROUNDS))
            pe.wait_ge(looked_copied, len(ROUNDS))
            turn(0, 0, 0, True)
            turn(0, 0, 1, True)
            tile(0, 0, 0, True)
            pe.wait_ge(looked_ready, len(ROUNDS))
            turn_dense()
            pe.wait_ge(split, WEIGHTS_STEP)
            pe.wait_ge(dense_copied, 2)
            tile(0, 1, 1, True)
            with pe.Fori(1, NT // 2 - 1) as k:
                tile(k, 0, 2, True)
                tile(k, 1, 2, True)
            tile(NT // 2 - 1, 0, 2, True)
            tile(NT // 2 - 1, 1, 2, False)
            for t in (NT, NT + 1):
                for what, back in MLP_AT.values():
                    if t - back < NT:
                        mlp(what, t - back, (t - back) % 2)


_INS = ["dense_ctx", "ids"] + [f"tbl_{i}" for i in range(TABLES)] + [
    "r_x0", "W_top1", "b_top1", "W_top2", "b_top2", "W_top3", "L0_rec_w", "L0_rec_alpha", "L0_rec_hv"]


def kernel(**inputs):
    import numpy as _np
    import concourse.bacc as _bacc
    from concourse import mybir as _mybir
    from concourse.bass_utils import run_bass_kernel_spmd as _run

    nc = _bacc.Bacc("TRN2", target_bir_lowering=False, num_devices=1)
    arrays, args = {}, {}
    for name in _INS:
        a = _np.ascontiguousarray(inputs[name])
        arrays[f"in_{name}"] = a
        args[name] = nc.dram_tensor(f"in_{name}", a.shape, _mybir.dt.from_np(a.dtype), kind="ExternalInput").ap()
    parts, const_at, at = [], {}, 0
    for name, table in constants().items():
        part = table.reshape(P, -1)
        const_at[name] = (at, part.shape[1])
        at += part.shape[1]
        parts.append(part)
    arrays["in_consts"] = _np.concatenate(parts, axis=1)
    consts = nc.dram_tensor("in_consts", arrays["in_consts"].shape, _mybir.dt.float32, kind="ExternalInput").ap()
    out = nc.dram_tensor("out_y", (BATCH, 1), _mybir.dt.float32, kind="ExternalOutput").ap()
    interaction_tower(nc, args["dense_ctx"], args["ids"], [args[f"tbl_{i}"] for i in range(TABLES)], args["r_x0"],
                      args["W_top1"], args["b_top1"], args["W_top2"], args["b_top2"], args["W_top3"],
                      args["L0_rec_w"], args["L0_rec_alpha"], args["L0_rec_hv"], consts, const_at, out)
    r = _run(nc, [arrays], core_ids=[0])
    return r.results[0]["out_y"]
```

```python
from contextlib import ExitStack

import concourse.bass as bass
import numpy as np
from concourse import mybir

F32 = mybir.dt.float32
F32R = mybir.dt.float32r
F16 = mybir.dt.float16
BF16 = mybir.dt.bfloat16
I32 = mybir.dt.int32
ALU = mybir.AluOpType
ACT = mybir.ActivationFunctionType

P = 128
BATCH = 2048
TABLES = 16
F = 39
FP = 40
D = 16
K = 16
H = 16
EMB = TABLES * D
R = 8
FC = P // R
TB = 256
BT = TB // P
NT = BATCH // TB
HALF = 8
QUADS = 4
STEPS = 10
NPROD = 4
N1, N2 = 512, 256
PRODS = 10
USES = 4
CHUNK_A, CHUNK_B, CHUNK_C = range(3)
CHUNKS = [(CHUNK_C, 2 * FC, F - 2 * FC), (CHUNK_A, 0, FC), (CHUNK_B, FC, FC)]
KINDS = [(zt, CHUNK_C, None) for zt in range(2)]
KINDS += [(zt, chunk, odd) for chunk in (CHUNK_A, CHUNK_B) for zt in range(2) for odd in range(2)]
LAST_OF = [STEPS - 3, STEPS - 1]
MLP_AT = {0: [("L2 1", 2)], 2: [("L3", 2)], 3: [("L1 0", 1)], 4: [("L1 1", 1)], 5: [("L1 2", 1)], 6: [("L1 3", 1)],
          9: [("L2 0", 1)]}
MLP = ["L1 0", "L1 1", "L1 2", "L1 3", "L2 0", "L2 1", "L3"]
MLP_AT_LAST = {0: [("L2 1", 2)], 2: [("L3", 2)], 3: [(what, 1) for what in MLP[:4]], 5: [("L2 0", 1), ("L2 1", 1)],
               7: [("L3", 1)]}
LAG = 2
SMALL = [13, 14, 9, 1, 15]
GATHERED = [i for i in range(TABLES) if i not in SMALL]
GATHERS = [[i for i in GATHERED if i <= 6], [i for i in GATHERED if 6 < i <= 13], [i for i in GATHERED if i > 13]]
ROWS = 125
TABLE_ROWS = [125000, 1250, 125000, 1000, 12500, 125000, 1000, 1250, 125000, 1000, 12500, 1000, 12500, 1250, 1250, 1250]
CHUNKS_OF = [rows // 2 // ROWS for rows in TABLE_ROWS]
PARTS = 3
HB = BATCH // 2
ROUNDS = [(half, i) for half in range(2) for i in SMALL]
NR = len(ROUNDS)
HOTS_BEFORE = [sum(CHUNKS_OF[i] for _, i in ROUNDS[:r]) for r in range(NR + 1)]
AHEAD = 3
W_ROUND = NR - 4
CUT_ROUND = W_ROUND - 2
DENSE_ROUND = W_ROUND
NIDS = 4
NHOT = 12
IDS_STEP = 5
TABLE_STEP = IDS_STEP + 2 * PARTS - 1
TABLES_STEP = TABLE_STEP + 2 * PARTS - 1
HALVES_STEP = TABLES_STEP + 1
CUT_STEP = HALVES_STEP + 4
DENSE_STEP = CUT_STEP + 2 * PARTS - 1 + 2
W1D_STEP = DENSE_STEP + 2 * PARTS - 1
WEIGHTS_STEP = W1D_STEP + 2
N_SMALL_LOADS = 5
N_WEIGHT_LOADS = 2 * HALF + 4
DENSE_PARTS = [0, 0, 0, 1, 1, 2]
W_PARTS = [0, 1, 2, 0, 1, 0]


def first_embedding(f):
    first, count, m, step = next(r for r in RUNS if r[0] <= f < r[0] + r[1])
    return m + step * (f - first)


def feature_runs():
    def fits(f, m):
        return 256 * f // F >= m >= 0 and (256 * f + 255) // F < m + R <= EMB
    runs, f = [], 0
    while f < F:
        end = min(F, FC * (f // FC + 1))
        best = (f, 0, 0, 0)
        for step in range(R):
            for m in range(256 * f // F, max(0, 256 * f // F - 2) - 1, -1):
                n = 0
                while f + n < end and fits(f + n, m + step * n):
                    n += 1
                if n > best[1]:
                    best = (f, n, m, step)
        runs.append(best)
        f += best[1]
    return runs


RUNS = feature_runs()


def constants():
    ident = np.eye(P, dtype=np.float32)
    groups = FP // 8
    below = np.zeros((P, groups, D), np.float32)
    above = np.zeros((P, groups, D), np.float32)
    slot = np.zeros((P, groups, 2, 8 * R), np.float32)
    for n in range(16 * F):
        g, row, f = n // P, n % P, n // 16
        low, high = 16 * n // F, (16 * n + 15) // F
        for d in range(D):
            (below if (16 * n + d) // F == low else above)[row, g, d] = 1.0
        for side, m in enumerate((low, high)):
            slot[row, g, side, R * (f % 8) + m - first_embedding(f)] = 1.0
    block = np.kron(np.eye(8, dtype=np.float32), np.ones((H, 1), np.float32))
    rows = {n: np.add.outer(float(n) * np.arange(P), np.arange(n)).astype(np.float32) for n in set(CHUNKS_OF)}
    half_rows = np.broadcast_to(np.array(TABLE_ROWS, np.float32) / 2, (P, TABLES))
    combine = np.zeros((P, 2 * D), np.float32)
    for i in range(2):
        for part in range(PARTS):
            for d in range(D):
                combine[(i * PARTS + part) * D + d, D * i + d] = 1.0
    return {"rows4": rows[4], "rows5": rows[5], "half_rows": half_rows, "combine": combine,
            "ident": ident, "below": below, "above": above, "slot": slot, "block": block}


def interaction_tower(nc, dense_ctx, ids, tables, x0, w_top1, b_top1, w_top2, b_top2, w_top3,
                      w, alpha, hv, consts, const_at, out):
    G = FP // 8
    NALPHA = 16 * F
    with ExitStack() as ctx:
        def sb(name, shape, dt=F32):
            return ctx.enter_context(nc.sbuf_tensor(name, shape, dt))

        def bank(name, shape):
            return ctx.enter_context(nc.psum_tensor(name, shape, F32))

        def sem(name):
            return ctx.enter_context(nc.semaphore(name))

        assert [table.shape[0] for table in tables] == TABLE_ROWS
        const = sb("const", [P, consts.shape[1]])

        def const_view(name, *dims):
            a, n = const_at[name]
            v = const[:, a:a + n]
            if len(dims) == 2:
                return v.rearrange("p (a b) -> p a b", a=dims[0])
            if len(dims) == 3:
                return v.rearrange("p (a b c) -> p a b c", a=dims[0], b=dims[1])
            return v

        ident = const_view("ident")
        below = const_view("below", G, D)
        above = const_view("above", G, D)
        slot = const_view("slot", G, 2, 8 * R)
        block_mask = const_view("block")
        row_of = {4: const_view("rows4"), 5: const_view("rows5")}
        half_rows = const_view("half_rows")
        ident_b = sb("ident_b", [P, P], BF16)
        ident_h = sb("ident_h", [P, P], F16)
        combine_b = sb("combine_b", [P, 2 * D], BF16)
        w1z_hi = sb("w1z_hi", [P, 2, N1], F32R)
        w1z_lo = sb("w1z_lo", [P, 2, N1], F32R)
        w2_hi = sb("w2_hi", [P, N1 // P, N2], F32R)
        w2_lo = sb("w2_lo", [P, N1 // P, N2], F32R)
        w1d_in = sb("w1d_in", [P, D * N1 // P])
        w1d_part = sb("w1d_part", [P, PARTS, D * N1 // P], BF16)
        w1d_six = sb("w1d_six", [len(W_PARTS) * D, N1], BF16)
        w3_in = sb("w3_in", [P, N2 // P])
        w3 = sb("w3", [P, N2 // P, 32])
        b1 = sb("b1", [P, N1 // P])
        b2 = sb("b2", [P, N2 // P])
        hv_col = sb("hv_col", [P, 2])
        w_rows = sb("w_rows", [P, 2, D])
        alpha_rows = sb("alpha_rows", [P, G, K])
        whv_diag = sb("whv_diag", [P, 2, P])
        alpha_slot = sb("alpha_slot", [P, 2, FP * R])
        m_ab = sb("m_ab", [P, 2, H, 32])
        m_c = sb("m_c", [P, H // 2, 32])
        dense_in = sb("dense_in", [P, NT * BT, D])
        dense_six = sb("dense_six", [P, NT * BT, len(DENSE_PARTS), D], BF16)
        dense_t = sb("dense_t", [len(DENSE_PARTS) * D, NT, TB], BF16)
        first_chunk = {}
        for i in SMALL:
            first_chunk[i] = sum(2 * CHUNKS_OF[j] for j in SMALL[:SMALL.index(i)])
        n_chunks = sum(2 * CHUNKS_OF[i] for i in SMALL)
        ids_all = sb("ids_all", [P, NT * BT, TABLES], I32)
        ids_h = sb("ids_h", [P, NT * BT, TABLES], F16)
        small = sb("small", [ROWS, n_chunks, D])
        small_parts = sb("small_parts", [ROWS, n_chunks, PARTS, D], BF16)
        in_half = sb("in_half", [P, 2, NT * BT, TABLES])
        x_in = sb("x_in", [P, 2, BT, F * H])
        emb = sb("emb", [P, NT * BT, EMB])
        emb_slot = sb("emb_slot", [P, 2, BT, FP * R])
        prod_ab = sb("prod_ab", [P, 2, 2, BT, H, P])
        prod_c = sb("prod_c", [P, 2, BT, H, P // 2])
        prod_t = sb("prod_t", [P, NPROD, QUADS, TB])

        def words(p, chunk, at, n):
            return prod_ab[:, p, chunk].rearrange("p c h j -> p (c h j)")[:, at:at + n]

        transposed = prod_t[:].rearrange("p b q n -> p (b q n)")
        ids_b = transposed[:, 0:2 * HB].bitcast(F16).rearrange("p (r n) -> p r n", r=NIDS)
        looked_t = transposed[:, 2 * HB:3 * HB].bitcast(BF16).rearrange("p (i n) -> p i n", i=2)
        small_rest = words(0, 0, 0, 2 * n_chunks * D)[0:ROWS].rearrange("p (j c d) -> p j c d", j=2, d=D)
        dense_rest = words(0, 0, 2 * HB, 2 * NT * BT * D).rearrange("p (j c d) -> p j c d", j=2, d=D)
        w1d_rest = words(1, 1, 2048 - 2 * D * N1 // P, 2 * D * N1 // P).rearrange("p (j n) -> p j n", j=2)
        n_cut = 2 * G * K * D
        alpha_cut = words(0, 1, 0, n_cut).rearrange("p (i g k d) -> p i g k d", i=2, g=G, k=K)
        w_diag = words(0, 1, n_cut, 2 * P).rearrange("p (z a b) -> p z a b", z=2, a=8)
        picked = words(0, 1, n_cut + 2 * P, 2 * 2 * D * HB // P).rearrange("p (j c i d) -> p j c i d", j=2, i=2, d=D)
        alpha_by_slot = words(0, 1, n_cut + 2 * P + 4 * D * HB // P, 3 * 2 * P).rearrange("p (q n) -> p q n", q=3)
        ids_f = words(1, 0, 0, NT * BT * TABLES).rearrange("p (c s) -> p c s", s=TABLES)
        lower_rows = words(1, 0, NT * BT * TABLES, NT * BT * TABLES).rearrange("p (c s) -> p c s", s=TABLES)
        hot = prod_ab[:, 1].rearrange("p i c h j -> p (i c h j)")[:, 0:NHOT * HB // 2].bitcast(BF16).rearrange("p (i n) -> p i n", n=HB)
        w1z = words(1, 1, 2048, 2 * N1).rearrange("p (z n) -> p z n", z=2)
        w2 = words(1, 1, 2048 + 2 * N1, N1 // P * N2).rearrange("p (m n) -> p m n", n=N2)
        z_sb = sb("z_sb", [P, 2, 2, TB])
        z_hi = sb("z_hi", [P, 2, 2, TB], F32R)
        z_lo = sb("z_lo", [P, 2, 2, TB], F32R)
        h1 = sb("h1", [P, N1 // P, TB])
        h1_hi = sb("h1_hi", [P, N1 // P, TB], F32R)
        h1_lo = sb("h1_lo", [P, N1 // P, TB], F32R)
        h2 = sb("h2", [P, N2 // P, TB])
        y = sb("y", [P, NT, TB // QUADS])

        turned = [bank(f"turned{i}", [P, QUADS, TB]) for i in range(2)]
        z_banks = bank("z_banks", [P, 2, 512])
        z_ps = [z_banks[:, i] for i in range(2)]
        shared = [bank(f"shared{i}", [P, 2, TB]) for i in range(2)]

        small_loaded = sem("small_loaded")
        const_loaded = sem("const_loaded")
        dense_loaded = sem("dense_loaded")
        weights_loaded = sem("weights_loaded")
        w1d_loaded = sem("w1d_loaded")
        x_loaded = [sem(f"x_loaded{i}") for i in range(2)]
        gathered = [[sem(f"gathered{i}_{c}") for c in range(3)] for i in range(2)]
        table_loaded = [sem(f"table_loaded{i}") for i in range(2)]
        tables_loaded = [sem(f"tables_loaded{i}") for i in range(2)]
        ids_here = sem("ids_here")
        split = sem("split")
        split_act = sem("split_act")
        spread = sem("spread")
        spread_copied = sem("spread_copied")
        hot_ready = sem("hot_ready")
        hot_used = sem("hot_used")
        first_looked = sem("first_looked")
        looked_copied = sem("looked_copied")
        turned_back = sem("turned_back")
        halves_picked = sem("halves_picked")
        looked_ready = sem("looked_ready")
        dense_turned = sem("dense_turned")
        dense_copied = sem("dense_copied")
        h1_kept = sem("h1_kept")
        lo_ready = sem("lo_ready")
        cleared = sem("cleared")
        bf16_ready = sem("bf16_ready")
        w3_cleared = sem("w3_cleared")
        setup_pe = sem("setup_pe")
        alpha_summed = sem("alpha_summed")
        alpha_turned = sem("alpha_turned")
        alpha_copied = sem("alpha_copied")
        setup_act = sem("setup_act")
        slotted = sem("slotted")
        prod_ready = sem("prod_ready")
        turned_full = sem("turned_full")
        copied = sem("copied")
        z_step = sem("z_step")
        z_drained = sem("z_drained")
        shared_full = sem("shared_full")
        shared_drained = sem("shared_drained")
        y_stored = sem("y_stored")

        out_rows = out.rearrange("(t q n) o -> q t (n o)", t=NT, q=QUADS)
        x_rows = x0.rearrange("(t c p) f h -> t p c (f h)", c=BT, p=P)
        dense_rows = dense_ctx.rearrange("(c p) s -> p c s", p=P)
        w1_rows = w_top1[0:K * H, :].rearrange("(k z hh) n -> z hh k n", z=2, hh=HALF)

        block = ctx.enter_context(nc.Block())

        def windows(values, m, count, step):
            (pstep, pn), (cstep, cn), _ = values.ap
            return bass.AP(values.tensor, values.offset + m, [[pstep, pn], [cstep, cn], [step, count], [1, R]])

        def at_tile(rows, t):
            if isinstance(t, int):
                return rows[t]
            return rows[bass.ds(t, 1)].squeeze(0)

        def flat(tile):
            return tile[:].rearrange("p a b -> p (a b)")

        def load_tables(queue, j):
            for i in SMALL:
                at = first_chunk[i]
                rows = slice(TABLE_ROWS[i] // 2 * j, TABLE_ROWS[i] // 2 * (j + 1))
                queue.dma_start(small[:, at + j:at + 2 * CHUNKS_OF[i]:2],
                                tables[i][rows].rearrange("(p c) d -> p c d", p=ROWS)).then_inc(
                                    (tables_loaded if i != SMALL[0] else table_loaded)[j], 16)

        @block.sync
        def _(sp):
            def load(k, p, again):
                t = 2 * k + p
                if again:
                    sp.wait_ge(prod_ready, PRODS * (t - 1))
                sp.dma_start(x_in[:, p], at_tile(x_rows, t)).then_inc(x_loaded[p], 16)

            sp.dma_start(ids_all[:], ids.rearrange("(c p) s -> p c s", p=P)).then_inc(ids_here, 16)
            sp.dma_start(const[:], consts).then_inc(const_loaded, 16)
            load_tables(sp, 0)
            with nc.allow_non_contiguous_dma(reason="small vectors, one element to a partition"):
                sp.wait_ge(cleared, 2)
                sp.dma_start(alpha_rows[:, 0:NALPHA // P],
                              alpha[0:P * (NALPHA // P), :].rearrange("(g p) k -> p g k", p=P)).then_inc(small_loaded, 16)
                sp.dma_start(alpha_rows[0:NALPHA % P, NALPHA // P],
                              alpha[P * (NALPHA // P):NALPHA, :]).then_inc(small_loaded, 16)
                sp.dma_start(w_rows[:], w.rearrange("(z k) h d -> z (k h) d", z=2).rearrange("z q d -> q z d")).then_inc(small_loaded, 16)
                hv_rows = hv.rearrange("(z k) d o -> z (k d) o", z=2)
                for z in range(2):
                    sp.dma_start(hv_col[:, z:z + 1], hv_rows[z]).then_inc(small_loaded, 16)
            sp.dma_start(dense_in[:], dense_rows).then_inc(dense_loaded, 16)
            sp.dma_start(w1d_in[:], w_top1[K * H:K * H + D, :].rearrange("s (c n) -> (s c) n", c=P // D)).then_inc(dense_loaded, 16)
            load(0, 0, False)
            with nc.allow_non_contiguous_dma(reason="small vectors, one element to a partition"):
                for z in range(2):
                    for hh in range(HALF):
                        sp.dma_start(w1z[K * hh:K * (hh + 1), z], w1_rows[z, hh]).then_inc(weights_loaded, 16)
                sp.dma_start(w2, w_top2.rearrange("(m p) n -> p m n", p=P)).then_inc(weights_loaded, 16)
                sp.dma_start(w3_in[:], w_top3.rearrange("(m p) o -> p (m o)", p=P)).then_inc(weights_loaded, 16)
                sp.dma_start(b1[:], b_top1.rearrange("(m p) -> p m", p=P)).then_inc(weights_loaded, 16)
                sp.dma_start(b2[:], b_top2.rearrange("(m p) -> p m", p=P)).then_inc(weights_loaded, 16)
            load(0, 1, False)
            sp.wait_ge(split, W1D_STEP)
            for i, part in enumerate(W_PARTS):
                sp.dma_start(w1d_six[D * i:D * (i + 1)], w1d_part[:, part]).then_inc(w1d_loaded, 16)
            with sp.Fori(1, NT // 2) as k:
                load(k, 0, True)
                load(k, 1, True)

        @block.gpsimd
        def _(pool):
            pool.wait_ge(ids_here, 16)
            for t in range(NT):
                k, p = divmod(t, 2)
                for chunk in range(3):
                    if k and GATHERS[chunk]:
                        pool.wait_ge(gathered[p][chunk], 16 * len(GATHERS[chunk]) * BT * k)
                    for s in GATHERS[chunk]:
                        for c in range(BT * t, BT * (t + 1)):
                            pool.indirect_dma_start(
                                emb[:, c, D * s:D * (s + 1)], None, tables[s],
                                bass.IndirectOffsetOnAxis(ids_all[:, c, s:s + 1], 0)).then_inc(gathered[p][chunk], 16)

        @block.vector
        def _(dve):
            done = [0]

            def step(instruction):
                done[0] += 1
                instruction.then_inc(split, 1)
                dve.wait_ge(split, done[0])

            def three_parts(source, rest, part):
                for i in range(PARTS):
                    step(nc.vector.tensor_copy(part(i), source))
                    if i < PARTS - 1:
                        step(nc.vector.tensor_tensor(rest(i), source, part(i), ALU.subtract))
                        source = rest(i)

            nc.vector.memset(m_c[:], 0.0).then_inc(cleared, 1)
            nc.vector.memset(alpha_rows[:], 0.0).then_inc(cleared, 1)
            nc.vector.memset(m_ab[:], 0.0).then_inc(cleared, 1)
            nc.vector.memset(prod_c[:, :, :, :, R * (F - 2 * FC):], 0.0).then_inc(cleared, 1)
            dve.wait_ge(const_loaded, 16)
            step(nc.vector.tensor_copy(ident_h[:], ident))
            dve.wait_ge(ids_here, 16)
            step(nc.vector.tensor_copy(ids_f[:], ids_all[:]))
            bound = half_rows.unsqueeze(1).broadcast_to([P, NT * BT, TABLES])
            step(nc.vector.tensor_tensor(in_half[:, 1], ids_f, bound, ALU.is_ge))
            step(nc.vector.tensor_tensor(lower_rows, in_half[:, 1], bound, ALU.mult))
            step(nc.vector.tensor_tensor(ids_h[:], ids_f, lower_rows, ALU.subtract))
            assert done[0] == IDS_STEP

            def one_hots(r):
                chunks = CHUNKS_OF[ROUNDS[r][1]]
                dve.wait_ge(spread_copied, r + 1)
                for chunk in range(chunks):
                    n = HOTS_BEFORE[r] + chunk
                    if n >= NHOT:
                        dve.wait_ge(hot_used, n - NHOT + 1)
                    nc.vector.tensor_scalar(hot[0:ROWS, n % NHOT], ids_b[0:ROWS, r % NIDS],
                                            row_of[chunks][0:ROWS, chunk:chunk + 1], None,
                                            ALU.is_equal).then_inc(hot_ready, 1)

            def keep_looked(r):
                half, i = ROUNDS[r]
                n = HB // P
                dve.wait_ge(turned_back, r + 1)
                nc.vector.tensor_tensor(
                    picked[:, r % 2], shared[r % 2][:, 0].rearrange("p (c i d) -> p c i d", i=2, d=D),
                    in_half[:, :, n * half:n * (half + 1), i].rearrange("p i c -> p c i").unsqueeze(3).broadcast_to([P, n, 2, D]),
                    ALU.mult).then_inc(halves_picked, 1)
                dve.wait_ge(halves_picked, r + 1)
                nc.vector.tensor_tensor(emb[:, n * half:n * (half + 1), D * i:D * (i + 1)],
                                        picked[:, r % 2, :, 0], picked[:, r % 2, :, 1], ALU.add).then_inc(looked_ready, 1)

            def cut_alpha():
                dve.wait_ge(small_loaded, 16 * N_SMALL_LOADS)
                for z in range(2):
                    step(nc.vector.tensor_tensor(
                        w_diag[:, z], w_rows[:, z].unsqueeze(1).broadcast_to([P, 8, D]),
                        block_mask.unsqueeze(2).broadcast_to([P, 8, D]), ALU.mult))
                for side, mask in enumerate((below, above)):
                    step(nc.vector.tensor_tensor(
                        alpha_cut[:, side], alpha_rows[:].unsqueeze(3).broadcast_to([P, G, K, D]),
                        mask.unsqueeze(2).broadcast_to([P, G, K, D]), ALU.mult))
                assert done[0] == CUT_STEP

            def split_dense():
                dve.wait_ge(dense_loaded, 32)
                six = [DENSE_PARTS.index(j) for j in range(PARTS)]
                three_parts(dense_in[:], lambda j: dense_rest[:, j], lambda j: dense_six[:, :, six[j]])
                step(nc.vector.tensor_copy(dense_six[:, :, 1:3], dense_six[:, :, 0:1].broadcast_to([P, NT * BT, 2, D])))
                step(nc.vector.tensor_copy(dense_six[:, :, 4], dense_six[:, :, 3]))
                assert done[0] == DENSE_STEP

            def split_weights():
                three_parts(w1d_in[:], lambda j: w1d_rest[:, j], lambda j: w1d_part[:, j])
                assert done[0] == W1D_STEP
                dve.wait_ge(split_act, 3)
                step(nc.vector.tensor_tensor(w1z_lo[:], w1z, w1z_hi[:].bitcast(F32), ALU.subtract))
                step(nc.vector.tensor_tensor(w2_lo[:], w2, w2_hi[:].bitcast(F32), ALU.subtract))
                assert done[0] == WEIGHTS_STEP

            def z_low(k, p):
                t = 2 * k + p
                dve.wait_ge(z_drained, 2 * (t + 1))
                nc.vector.tensor_tensor(z_lo[:, p], z_sb[:, p], z_hi[:, p].bitcast(F32),
                                        ALU.subtract).then_inc(lo_ready, 1)

            def h1_low(t, i):
                dve.wait_ge(shared_drained, USES * t + 1 + i)
                part = slice(2 * i, 2 * i + 2)
                nc.vector.tensor_tensor(h1_lo[:, part], h1[:, part], h1_hi[:, part].bitcast(F32),
                                        ALU.subtract).then_inc(lo_ready, 1)

            def products(k, p, again, last=False):
                t = 2 * k + p
                t_is_first = not again and p == 0
                if again:
                    dve.wait_ge(prod_ready, PRODS * (t - 1))
                embeddings = emb[:, BT * t:BT * (t + 1)] if isinstance(t, int) else emb[:, bass.ds(BT * t, BT)]
                slots_done = 0
                for chunk, feature, count in CHUNKS:
                    if GATHERS[chunk]:
                        dve.wait_ge(gathered[p][chunk], 16 * len(GATHERS[chunk]) * BT * (k + 1))
                    for f, n, m, stride in RUNS:
                        if feature <= f < feature + count:
                            nc.vector.tensor_copy(
                                emb_slot[:, p, :, R * f:R * (f + n)].rearrange("p c (f r) -> p c f r", r=R),
                                windows(embeddings, m, n, stride)).then_inc(slotted, 1)
                            slots_done += 1
                    if chunk == CHUNK_C:
                        dve.wait_ge(x_loaded[p], 16 * (k + 1))
                    dve.wait_ge(slotted, len(RUNS) * t + slots_done)
                    if again:
                        dve.wait_ge(turned_full, STEPS * (t - 2) + {CHUNK_C: 2, CHUNK_A: 6, CHUNK_B: 10}[chunk])
                    for heads in ([slice(0, H)] if chunk == CHUNK_C else [slice(0, HALF), slice(HALF, H)]):
                        for c in range(BT):
                            to = prod_c[:, p, c, heads, 0:R * count] if chunk == CHUNK_C else prod_ab[:, p, chunk, c, heads]
                            rows = x_in[:, p, c].rearrange("p (f h) -> p h f", h=H)[:, heads, feature:feature + count]
                            slots = emb_slot[:, p, c, R * feature:R * (feature + count)]
                            n = heads.stop - heads.start
                            nc.vector.tensor_tensor(
                                to.rearrange("p h (f r) -> p h f r", r=R),
                                rows.unsqueeze(3).broadcast_to([P, n, count, R]),
                                slots.unsqueeze(1).broadcast_to([P, n, R * count]).rearrange("p h (f r) -> p h f r", r=R),
                                ALU.mult).then_inc(prod_ready, 1)
                        if last and chunk == CHUNK_B and heads.start == 0:
                            for i in range(2):
                                h1_low(t - 1, i)
                    if t_is_first and chunk == CHUNK_A:
                        keep_looked(NR - 2)
                        keep_looked(NR - 1)
                        dve.wait_ge(alpha_turned, 1)
                    if chunk == CHUNK_C and again:
                        for i in range(2):
                            h1_low(t - 2, i)
                    if chunk == CHUNK_A and not again and p:
                        split_weights()
                    if chunk == CHUNK_A and (again or p):
                        z_low(k if p else k - 1, 1 - p)

            def split_tables(tables, loaded):
                for j in range(2):
                    dve.wait_ge(loaded[j], 16 * len(tables))
                chunks = slice(first_chunk[tables[0]], first_chunk[tables[-1]] + 2 * CHUNKS_OF[tables[-1]])
                three_parts(small[:, chunks], lambda j: small_rest[:, j, chunks], lambda j: small_parts[:, chunks, j])

            split_tables(SMALL[:1], table_loaded)
            one_hots(0)
            split_tables(SMALL[1:], tables_loaded)
            assert done[0] == TABLES_STEP
            step(nc.vector.tensor_scalar(in_half[:, 0], in_half[:, 1], -1.0, 1.0, ALU.mult, ALU.add))
            assert done[0] == HALVES_STEP
            for r in range(1, NR):
                one_hots(r)
                if r >= 2:
                    keep_looked(r - 2)
                if r == CUT_ROUND:
                    cut_alpha()
                if r == DENSE_ROUND:
                    split_dense()
            dve.wait_ge(looked_ready, len(SMALL))
            products(0, 0, False)
            dve.wait_ge(hot_used, HOTS_BEFORE[-1])
            dve.wait_ge(looked_ready, NR)
            products(0, 1, False)
            with dve.Fori(1, NT // 2 - 1) as k:
                products(k, 0, True)
                products(k, 1, True)
            products(NT // 2 - 1, 0, True)
            products(NT // 2 - 1, 1, True, last=True)
            t, p = NT - 1, 1
            for zt in range(2):
                dve.wait_ge(z_drained, 2 * t + zt + 1)
                nc.vector.tensor_tensor(z_lo[:, p, zt], z_sb[:, p, zt], z_hi[:, p, zt].bitcast(F32),
                                        ALU.subtract).then_inc(lo_ready, 1)
            for i in range(2):
                dve.wait_ge(shared_full, USES * t + 1 + i)
                m = 2 * i + 1
                for to in (h1, h1_hi):
                    nc.vector.tensor_scalar(to[:, m], turned[i][:, 2], b1[:, m:m + 1], 0.0, ALU.add, ALU.max).then_inc(h1_kept, 1)
                dve.wait_ge(h1_kept, 2 * (i + 1))
                h1_low(t, i)
            dve.wait_ge(shared_full, USES * t + 3)
            nc.vector.tensor_scalar(h2[:, 1], shared[1][:, 0], b2[:, 1:2], 0.0, ALU.add, ALU.max).then_inc(h1_kept, 1)

        @block.scalar
        def _(act):
            act.wait_ge(cleared, 1)
            nc.scalar.activation(w3[:], m_c[:, 0:N2 // P], ACT.Copy).then_inc(w3_cleared, 1)
            load_tables(act, 1)
            act.wait_ge(const_loaded, 16)
            nc.scalar.activation(ident_b[:], ident, ACT.Copy).then_inc(bf16_ready, 1)
            nc.scalar.activation(combine_b[:], const_view("combine"), ACT.Copy).then_inc(bf16_ready, 1)

            def copy_spread(r):
                act.wait_ge(spread, r + 1)
                if r >= NIDS:
                    act.wait_ge(hot_ready, HOTS_BEFORE[r - NIDS + 1])
                nc.scalar.activation(ids_b[:, r % NIDS], flat(turned[r % 2]), ACT.Copy).then_inc(spread_copied, 1)

            def copy_looked(r, part):
                n = 2 * PARTS * D
                if part == 0:
                    act.wait_ge(first_looked, r + 1)
                else:
                    act.wait_ge(hot_used, HOTS_BEFORE[r + 1])
                if r >= 2:
                    act.wait_ge(turned_back, r - 1)
                nc.scalar.activation(looked_t[0:n, r % 2, 512 * part:512 * (part + 1)], z_ps[part][0:n], ACT.Copy).then_inc(
                    looked_copied, 1)

            def w_hv():
                act.wait_ge(setup_pe, 1)
                act.wait_ge(small_loaded, 16 * N_SMALL_LOADS)
                for z in range(2):
                    nc.scalar.activation(whv_diag[:, z], flat(turned[0])[:, 512 * z + 384:512 * z + 512], ACT.Copy,
                                         scale=hv_col[:, z:z + 1]).then_inc(setup_act, 1)

            def copy_alpha_sums():
                act.wait_ge(alpha_summed, 1)
                nc.scalar.activation(alpha_by_slot[:, 0:2], turned[0][:, 0:2], ACT.Copy).then_inc(alpha_copied, 1)
                nc.scalar.activation(alpha_by_slot[0:64, 2], turned[0][0:64, 2], ACT.Copy).then_inc(alpha_copied, 1)

            def copy_alpha():
                act.wait_ge(alpha_turned, 1)
                for z in range(2):
                    nc.scalar.activation(alpha_slot[:, z], flat(turned[0])[:, 512 * z:512 * z + FP * R], ACT.Copy).then_inc(alpha_copied, 1)

            def copy_dense():
                for i in range(2):
                    act.wait_ge(dense_turned, i + 1)
                    nc.scalar.activation(dense_t[:].rearrange("p t n -> p (t n)")[:, 4 * TB * i:4 * TB * (i + 1)],
                                         flat(turned[1])[0:len(DENSE_PARTS) * D, 512 * i:512 * (i + 1)].bitcast(BF16),
                                         ACT.Copy).then_inc(dense_copied, 1)

            def copy_m():
                act.wait_ge(setup_pe, 2)
                act.wait_ge(cleared, 3)
                m_view = [turned[0][:, i] for i in range(3)]
                for odd in range(2):
                    cols = slice(K * odd, K * (odd + 1))
                    for chunk in (CHUNK_A, CHUNK_B):
                        nc.scalar.activation(
                            m_ab[:, chunk, odd::2, cols],
                            m_view[chunk].rearrange("p (k h) -> p h k", h=H)[:, odd::2, :], ACT.Copy).then_inc(setup_act, 1)
                    rows = slice(64 * odd, 64 * (odd + 1))
                    nc.scalar.activation(
                        m_c[rows, :, cols],
                        m_view[CHUNK_C].rearrange("p (k h) -> p h k", h=H)[rows, odd::2, :], ACT.Copy).then_inc(setup_act, 1)

            def split_high():
                act.wait_ge(weights_loaded, 16 * N_WEIGHT_LOADS)
                nc.scalar.activation(w1z_hi[:], w1z, ACT.Copy).then_inc(split_act, 1)
                nc.scalar.activation(w2_hi[:], w2, ACT.Copy).then_inc(split_act, 1)
                act.wait_ge(w3_cleared, 1)
                nc.scalar.activation(w3[:, :, 0], w3_in[:], ACT.Copy).then_inc(split_act, 1)

            for r in range(AHEAD):
                copy_spread(r)
            for r in range(NR):
                if r + AHEAD < NR:
                    copy_spread(r + AHEAD)
                if r == W_ROUND:
                    w_hv()
                elif r == NR - 1:
                    copy_m()
                copy_looked(r, 0)
                if r == W_ROUND + 1:
                    copy_alpha_sums()
                elif r == W_ROUND + 2:
                    copy_alpha()
                copy_looked(r, 1)
                if r == W_ROUND:
                    split_high()
                elif r == W_ROUND + 2:
                    copy_dense()

            def copy_products(t, p, s, again):
                n = STEPS * t + s
                act.wait_ge(turned_full, n + 1)
                if again or s >= NPROD:
                    act.wait_ge(z_step, n - NPROD + 1)
                nc.scalar.activation(prod_t[:, (STEPS * p + s) % NPROD], turned[s % 2][:], ACT.Copy).then_inc(copied, 1)

            def drain_z(t, p, zt):
                act.wait_ge(z_step, STEPS * t + LAST_OF[zt] + 1)
                nc.scalar.activation(z_sb[:, p, zt], z_ps[zt][:, 0:TB], ACT.Copy)
                nc.scalar.activation(z_hi[:, p, zt], z_ps[zt][:, 0:TB], ACT.Copy).then_inc(z_drained, 1)

            def mlp_drain(what, t):
                use = USES * t
                if what in ("L1 1", "L1 3"):
                    m = int(what[3]) - 1
                    source = shared[m // 2]
                    act.wait_ge(shared_full, use + m // 2 + 1)
                    for i in range(2):
                        for to in (h1, h1_hi):
                            last = nc.scalar.activation(to[:, m + i], source[:, i], ACT.Relu, bias=b1[:, m + i:m + i + 1])
                    last.then_inc(shared_drained, 1)
                elif what == "L2 1":
                    act.wait_ge(shared_full, use + 3)
                    for i in range(2):
                        last = nc.scalar.activation(h2[:, i], shared[0][:, i], ACT.Relu, bias=b2[:, i:i + 1])
                    last.then_inc(shared_drained, 1)
                elif what == "L3":
                    act.wait_ge(shared_full, use + 4)
                    to = y[:, t] if isinstance(t, int) else y[:, bass.ds(t, 1)].squeeze(1)
                    nc.scalar.activation(to, shared[1][:, 0, 0:TB // QUADS], ACT.Copy).then_inc(shared_drained, 1)

            def tile(k, p, earlier, mlp_at=MLP_AT):
                t = 2 * k + p
                for s in range(STEPS):
                    copy_products(t, p, s, earlier)
                    if s == 1 and earlier:
                        drain_z(t - 1, 1 - p, 1)
                    for what, back in mlp_at.get(s - LAG, []):
                        if back <= earlier:
                            mlp_drain(what, t - back)
                drain_z(t, p, 0)

            tile(0, 0, 0)
            tile(0, 1, 1)
            with act.Fori(1, NT // 2 - 1) as k:
                tile(k, 0, 2)
                tile(k, 1, 2)
            tile(NT // 2 - 1, 0, 2)
            tile(NT // 2 - 1, 1, 2, MLP_AT_LAST)
            drain_z(NT - 1, 1, 1)
            t = NT - 1
            for i in range(2):
                act.wait_ge(shared_full, USES * t + 1 + i)
                for to in (h1, h1_hi):
                    last = nc.scalar.activation(to[:, 2 * i], turned[i][:, 0], ACT.Relu, bias=b1[:, 2 * i:2 * i + 1])
                last.then_inc(shared_drained, 1)
            act.wait_ge(shared_full, USES * t + 3)
            nc.scalar.activation(h2[:, 0], shared[0][:, 0], ACT.Relu, bias=b2[:, 0:1]).then_inc(shared_drained, 1)
            mlp_drain("L3", t)
            act.wait_ge(shared_drained, USES * NT)
            act.dma_start(out_rows, y[0:P:P // QUADS]).then_inc(y_stored, 16)
            act.wait_ge(y_stored, 16)

        @block.tensor
        def _(pe):
            mm = nc.tensor.matmul

            def spread_ids(r):
                half, i = ROUNDS[r]
                if r >= 2:
                    pe.wait_ge(spread_copied, r - 1)
                for c in range(HB // P):
                    last = mm(flat(turned[r % 2])[:, P * c:P * (c + 1)],
                              ids_h[:, HB // P * half + c, i:i + 1].broadcast_to([P, P]), ident_h[:],
                              start=True, stop=True)
                last.then_inc(spread, 1)

            def look_up(r, part):
                i = ROUNDS[r][1]
                if r:
                    pe.wait_ge(looked_copied, 2 * (r - 1) + part + 1)
                for chunk in range(CHUNKS_OF[i]):
                    n = HOTS_BEFORE[r] + chunk
                    if part == 0:
                        pe.wait_ge(hot_ready, n + 1)
                    at = first_chunk[i] + 2 * chunk
                    last = mm(z_ps[part][0:2 * PARTS * D, :],
                              small_parts[:, at:at + 2].rearrange("p i j d -> p (i j d)"),
                              hot[0:ROWS, n % NHOT, 512 * part:512 * (part + 1)],
                              start=chunk == 0, stop=chunk == CHUNKS_OF[i] - 1)
                    if part == 1:
                        last.then_inc(hot_used, 1)
                if part == 0:
                    last.then_inc(first_looked, 1)

            def turn_back(r):
                pe.wait_ge(looked_copied, 2 * (r + 1))
                if r == 0:
                    pe.wait_ge(bf16_ready, 2)
                if r >= 2:
                    pe.wait_ge(looked_ready, r - 1)
                for c in range(HB // P):
                    last = mm(shared[r % 2][:, 0, 2 * D * c:2 * D * (c + 1)],
                              looked_t[0:2 * PARTS * D, r % 2, P * c:P * (c + 1)],
                              combine_b[0:2 * PARTS * D], start=True, stop=True)
                last.then_inc(turned_back, 1)

            def turn_w():
                pe.wait_ge(split, CUT_STEP - 2)
                pe.wait_ge(spread_copied, NR)
                for z in range(2):
                    last = nc.tensor.transpose(flat(turned[0])[:, 512 * z + 384:512 * z + 512],
                                               w_diag[:, z].rearrange("p a b -> p (a b)"), ident)
                last.then_inc(setup_pe, 1)

            def sum_alpha():
                pe.wait_ge(setup_act, 2)
                pe.wait_ge(split, CUT_STEP)
                for q in range(3):
                    for side in range(2):
                        for g in range(2 * q, min(G, 2 * q + 2)):
                            last = mm(turned[0][64 * (g % 2):64 * (g % 2) + 64, q], slot[:, g, side],
                                      alpha_cut[:, side, g].rearrange("p k d -> p (k d)"),
                                      start=side == 0, stop=side == 1, tile_position=(0, 64 * (g % 2)))
                last.then_inc(alpha_summed, 1)

            def turn_alpha():
                pe.wait_ge(alpha_copied, 2)
                for z in range(2):
                    for q in range(3):
                        n = P if q < 2 else 64
                        last = nc.tensor.transpose(flat(turned[0])[:, 512 * z + P * q:512 * z + P * q + n],
                                                   alpha_by_slot[0:n, q, P * z:P * (z + 1)], ident[0:n, 0:n])
                last.then_inc(alpha_turned, 1)

            def make_m():
                pe.wait_ge(alpha_copied, 4)
                for z in range(2):
                    for chunk in (CHUNK_A, CHUNK_B):
                        mm(turned[0][:, chunk, P * z:P * (z + 1)], alpha_slot[:, z, P * chunk:P * (chunk + 1)], whv_diag[:, z],
                           start=True, stop=True)
                    for odd in range(2):
                        last = mm(turned[0][64 * odd:64 * (odd + 1), CHUNK_C, P * z:P * (z + 1)],
                                  alpha_slot[:, z, 2 * P:2 * P + 64], whv_diag[:, z], start=True, stop=True,
                                  tile_position=(0, 64 * odd))
                last.then_inc(setup_pe, 1)

            def turn_dense():
                pe.wait_ge(split, DENSE_STEP)
                pe.wait_ge(spread_copied, NR)
                for i in range(2):
                    for c in range(NT * BT // 2):
                        to = flat(turned[1])[0:len(DENSE_PARTS) * D, 512 * i:512 * (i + 1)].bitcast(BF16)
                        last = nc.tensor.transpose(to[:, P * c:P * (c + 1)],
                                                   dense_six[:, NT * BT // 2 * i + c].rearrange("p j d -> p (j d)"), ident_b[:])
                    last.then_inc(dense_turned, 1)

            def turn(k, p, s, first):
                t = 2 * k + p
                n = STEPS * t + s
                zt, chunk, odd = KINDS[s]
                if s % 2 == 0:
                    pe.wait_ge(prod_ready, PRODS * t + BT * (s // 2 + 1))
                if not first or s >= 2:
                    pe.wait_ge(copied, n - 1)
                for q in range(QUADS):
                    h = HALF * zt + 2 * q
                    for c in range(BT):
                        if chunk == CHUNK_C:
                            slots = prod_c[:, p, c, h:h + 2].rearrange("p h j -> p (h j)")
                        else:
                            slots = prod_ab[:, p, chunk, c, h + odd]
                        last = nc.tensor.transpose(turned[s % 2][:, q, P * c:P * (c + 1)], slots, ident)
                last.then_inc(turned_full, 1)

            def contract(k, p, s, first):
                t = 2 * k + p
                n = STEPS * t + s
                zt, chunk, odd = KINDS[s]
                pe.wait_ge(copied, n + 1)
                if s < 2 and not first:
                    pe.wait_ge(z_drained, 2 * (t - 1) + zt + 1)
                for q in range(QUADS):
                    h = HALF * zt + 2 * q
                    weights = m_c[:, h // 2] if chunk == CHUNK_C else m_ab[:, chunk, h + odd]
                    last = mm(z_ps[zt][32 * q:32 * (q + 1), 0:TB], weights,
                              prod_t[:, (STEPS * p + s) % NPROD, q],
                              start=s < 2, stop=s == LAST_OF[zt], tile_position=(0, 32 * q))
                last.then_inc(z_step, 1)

            def mlp(what, t, p):
                use = USES * t
                layer, m = what[:2], int((what + " 0").split()[1])
                cols = slice(P * m, P * (m + 1))
                if layer == "L1":
                    if m == 0 and isinstance(t, int) and t == 0:
                        pe.wait_ge(split, WEIGHTS_STEP)
                        pe.wait_ge(w1d_loaded, 16 * len(W_PARTS))
                        pe.wait_ge(looked_ready, NR)
                    if m == 0:
                        pe.wait_ge(lo_ready, 3 * t + 1)
                    if m % 2 == 0 and not (isinstance(t, int) and t == 0):
                        pe.wait_ge(shared_drained, use + m // 2 - 1)
                    to = shared[m // 2][:, m % 2]
                    mm(to, w1d_six[:, cols], dense_t[:, t] if isinstance(t, int) else dense_t[:, bass.ds(t, 1)].squeeze(1),
                       start=True, stop=False)
                    for n, (weights, z) in enumerate([(w1z_hi, z_hi), (w1z_lo, z_hi), (w1z_hi, z_lo)]):
                        for zt in range(2):
                            last = mm(to, weights[:, zt, cols], z[:, p, zt], start=False, stop=n == 2 and zt == 1)
                    if m % 2 == 1:
                        last.then_inc(shared_full, 1)
                elif layer == "L2":
                    if m == 0:
                        pe.wait_ge(lo_ready, 3 * t + 3)
                    for n, (weights, h) in enumerate([(w2_hi, h1_hi), (w2_lo, h1_hi), (w2_hi, h1_lo)]):
                        for i in range(N1 // P):
                            last = mm(shared[0][:, m], weights[:, i, cols], h[:, i],
                                      start=n == 0 and i == 0, stop=n == 2 and i == N1 // P - 1)
                    if m == 1:
                        last.then_inc(shared_full, 1)
                else:
                    pe.wait_ge(shared_drained, use + 3)
                    n = TB // QUADS
                    for i in range(N2 // P):
                        for q in range(QUADS):
                            last = mm(shared[1][32 * q:32 * (q + 1), 0, 0:n], w3[:, i], h2[:, i, n * q:n * (q + 1)],
                                      start=i == 0, stop=i == N2 // P - 1, tile_position=(0, 32 * q))
                    last.then_inc(shared_full, 1)

            def last_mlp():
                t, p = NT - 1, 1
                for i in range(2):
                    for m in (2 * i, 2 * i + 1):
                        mm(turned[i][:, 2 * (m % 2)], w1d_six[:, P * m:P * (m + 1)], dense_t[:, t], start=True, stop=False)
                    for zt in range(2):
                        for part in range(2):
                            if i == 0 and part == 0:
                                pe.wait_ge(z_drained, 2 * t + zt + 1)
                            elif i == 0:
                                pe.wait_ge(lo_ready, 3 * t + zt + 1)
                            z = (z_hi, z_lo)[part]
                            for m in (2 * i, 2 * i + 1):
                                for weights in ((w1z_hi, w1z_lo), (w1z_hi,))[part]:
                                    last = mm(turned[i][:, 2 * (m % 2)], weights[:, zt, P * m:P * (m + 1)], z[:, p, zt],
                                              start=False, stop=zt == 1 and part == 1)
                    last.then_inc(shared_full, 1)
                pe.wait_ge(shared_drained, USES * t)
                for i in range(2):
                    for part in range(2):
                        if part == 0:
                            pe.wait_ge(shared_drained, USES * t + i + 1)
                            pe.wait_ge(h1_kept, 2 * (i + 1))
                        else:
                            pe.wait_ge(lo_ready, 3 * t + 3 + i)
                        h = (h1_hi, h1_lo)[part]
                        for m in range(2):
                            for weights in ((w2_hi, w2_lo), (w2_hi,))[part]:
                                for j in (2 * i, 2 * i + 1):
                                    last = mm(shared[m][:, 0], weights[:, j, P * m:P * (m + 1)], h[:, j],
                                              start=i == 0 and part == 0 and weights is w2_hi and j == 0,
                                              stop=i == 1 and part == 1 and j == 3)
                last.then_inc(shared_full, 1)
                pe.wait_ge(h1_kept, 5)
                mlp("L3", t, p)

            def tile(k, p, earlier, following, mlp_at=MLP_AT):
                t = 2 * k + p
                nk, np_ = (k, 1) if p == 0 else (k + 1, 0)
                for s in range(STEPS):
                    if s + 2 < STEPS:
                        turn(k, p, s + 2, not earlier)
                    elif following:
                        turn(nk, np_, s + 2 - STEPS, False)
                    contract(k, p, s, not earlier)
                    for what, back in mlp_at.get(s, []):
                        if back <= earlier:
                            mlp(what, t - back, (p + back) % 2)

            pe.wait_ge(split, IDS_STEP)
            for r in range(AHEAD):
                spread_ids(r)
            pe.wait_ge(split, TABLE_STEP)
            for r in range(NR):
                if r + AHEAD < NR:
                    spread_ids(r + AHEAD)
                if r == W_ROUND:
                    turn_w()
                if r == 1:
                    pe.wait_ge(split, TABLES_STEP)
                if r == NR - 1:
                    make_m()
                look_up(r, 0)
                if r:
                    turn_back(r - 1)
                if r == W_ROUND + 1:
                    sum_alpha()
                elif r == W_ROUND + 2:
                    turn_alpha()
                look_up(r, 1)
                if r == W_ROUND + 2:
                    turn_dense()
            pe.wait_ge(setup_act, 8)
            turn(0, 0, 0, True)
            turn_back(NR - 1)
            pe.wait_ge(dense_copied, 2)
            turn(0, 0, 1, True)
            pe.wait_ge(looked_copied, 2 * NR)
            tile(0, 0, 0, True)
            tile(0, 1, 1, True)
            with pe.Fori(1, NT // 2 - 1) as k:
                tile(k, 0, 2, True)
                tile(k, 1, 2, True)
            tile(NT // 2 - 1, 0, 2, True)
            tile(NT // 2 - 1, 1, 2, False, MLP_AT_LAST)
            last_mlp()


_INS = ["dense_ctx", "ids"] + [f"tbl_{i}" for i in range(TABLES)] + [
    "r_x0", "W_top1", "b_top1", "W_top2", "b_top2", "W_top3", "L0_rec_w", "L0_rec_alpha", "L0_rec_hv"]


def kernel(**inputs):
    import numpy as _np
    import concourse.bacc as _bacc
    from concourse import mybir as _mybir
    from concourse.bass_utils import run_bass_kernel_spmd as _run

    nc = _bacc.Bacc("TRN2", target_bir_lowering=False, num_devices=1)
    arrays, args = {}, {}
    for name in _INS:
        a = _np.ascontiguousarray(inputs[name])
        arrays[f"in_{name}"] = a
        args[name] = nc.dram_tensor(f"in_{name}", a.shape, _mybir.dt.from_np(a.dtype), kind="ExternalInput").ap()
    parts, const_at, at = [], {}, 0
    for name, table in constants().items():
        part = table.reshape(P, -1)
        const_at[name] = (at, part.shape[1])
        at += part.shape[1]
        parts.append(part)
    arrays["in_consts"] = _np.concatenate(parts, axis=1)
    consts = nc.dram_tensor("in_consts", arrays["in_consts"].shape, _mybir.dt.float32, kind="ExternalInput").ap()
    out = nc.dram_tensor("out_y", (BATCH, 1), _mybir.dt.float32, kind="ExternalOutput").ap()
    interaction_tower(nc, args["dense_ctx"], args["ids"], [args[f"tbl_{i}"] for i in range(TABLES)], args["r_x0"],
                      args["W_top1"], args["b_top1"], args["W_top2"], args["b_top2"], args["W_top3"],
                      args["L0_rec_w"], args["L0_rec_alpha"], args["L0_rec_hv"], consts, const_at, out)
    r = _run(nc, [arrays], core_ids=[0])
    return r.results[0]["out_y"]
```
